# Optimizing a Trainium2 kernel written in Bass

```python
import numpy as np
import jax
import jax.numpy as jnp

def _softmax(x, axis=-1):
    return jax.nn.softmax(x, axis=axis)
def _gelu(x):
    return jax.nn.gelu(x, approximate=True)
def _silu(x):
    return jax.nn.silu(x)
def _sigmoid(x):
    return jax.nn.sigmoid(x)
def _layernorm(x, axis=-1, eps=1e-5):
    m = jnp.mean(x, axis=axis, keepdims=True)
    v = jnp.var(x, axis=axis, keepdims=True)
    return (x - m) / jnp.sqrt(v + eps)
def _scatter_add(tgt, idx, src, axis=0):
    return tgt.at[idx].add(src)
def _segment_sum(src, seg, n):
    return jax.ops.segment_sum(src, seg, n)

kernel_name = 'mk_conv_preact_d2_conv_nchw64_342b7c'

def setup_inputs(seed: int = 0):
    np.random.seed(seed)
    _w = jnp.asarray
    def _rec_inputs():
        import jax
        import jax.numpy as jnp
        _gk = jax.random.key(seed)
        x = -8.268e-05 + 0.9999 * jax.random.normal(jax.random.fold_in(_gk, 1), (16, 64, 224, 224), jnp.float32)
        return x
    x = _rec_inputs()
    def _L0_conv_setup():
        import jax, jax.numpy as jnp
        import numpy as np

        def _masked_conv(x, weight, bias, channel_mask, input_channel_mask):
            w_eff = weight * channel_mask.astype(weight.dtype)[:, None, None, None] * input_channel_mask.astype(weight.dtype)[None, :, None, None]
            y = jax.lax.conv_general_dilated(x, w_eff, window_strides=(1, 1), padding=((1, 1), (1, 1)), rhs_dilation=(1, 1), dimension_numbers=('NCHW', 'OIHW', 'NCHW'))
            b_eff = bias * channel_mask.astype(bias.dtype)
            return y + b_eff[None, :, None, None]
        key = jax.random.key(seed)
        k1, k2, k3, k4, k5 = jax.random.split(key, 5)
        N, Ci, Co, H, W, KH, KW = (16, 64, 64, 224, 224, 3, 3)
        x = jax.random.normal(k1, (N, Ci, H, W), dtype=jnp.float32)
        fan_in = Ci * KH * KW
        bound = 1.0 / np.sqrt(fan_in)
        weight = jax.random.normal(k2, (Co, Ci, KH, KW), dtype=jnp.float32) * bound
        bias = jax.random.uniform(k3, (Co,), minval=-bound, maxval=bound, dtype=jnp.float32)
        channel_mask = jax.random.randint(k4, (Co,), 0, 2).astype(jnp.bool_)
        input_channel_mask = jax.random.randint(k5, (Ci,), 0, 2).astype(jnp.bool_)
        return {'x': x, 'weight': weight, 'bias': bias, 'channel_mask': channel_mask, 'input_channel_mask': input_channel_mask}
    _L0_conv_all = _L0_conv_setup()
    _L0_conv_in = {k: v for k, v in _L0_conv_all.items() if k in ('weight', 'bias', 'channel_mask', 'input_channel_mask', )}
    del _L0_conv_all

    def _L1_conv_setup():
        import jax, jax.numpy as jnp
        import numpy as np
        B, C, H, W = (8, 64, 256, 256)
        SPLIT = 16
        K = 31
        PAD = K // 2
        DN = ('NCHW', 'OIHW', 'NCHW')

        def _dwconv(x, w, b, pad):
            y = jax.lax.conv_general_dilated(x, w, window_strides=(1, 1), padding=pad, dimension_numbers=DN, feature_group_count=w.shape[0])
            return y + b[None, :, None, None]
        key = jax.random.key(seed)
        ks = jax.random.split(key, 7)
        s = 0.05
        return {'x': jax.random.normal(ks[0], (B, C, H, W), jnp.float32), 'w_1xk': jax.random.normal(ks[1], (SPLIT, 1, 1, K), jnp.float32) * s, 'b_1xk': jax.random.normal(ks[2], (SPLIT,), jnp.float32) * s, 'w_kx1': jax.random.normal(ks[3], (SPLIT, 1, K, 1), jnp.float32) * s, 'b_kx1': jax.random.normal(ks[4], (SPLIT,), jnp.float32) * s, 'w1': jax.random.normal(ks[5], (C, C, 1, 1), jnp.float32) * s, 'b1': jax.random.normal(ks[6], (C,), jnp.float32) * s}
    _L1_conv_all = _L1_conv_setup()
    _L1_conv_in = {k: v for k, v in _L1_conv_all.items() if k in ('w_1xk', 'b_1xk', 'w_kx1', 'b_kx1', 'w1', 'b1', )}
    del _L1_conv_all

    return {
        "x": x,
        "L0_conv_weight": _L0_conv_in["weight"],
        "L0_conv_bias": _L0_conv_in["bias"],
        "L0_conv_channel_mask": _L0_conv_in["channel_mask"],
        "L0_conv_input_channel_mask": _L0_conv_in["input_channel_mask"],
        "L1_conv_w_1xk": _L1_conv_in["w_1xk"],
        "L1_conv_b_1xk": _L1_conv_in["b_1xk"],
        "L1_conv_w_kx1": _L1_conv_in["w_kx1"],
        "L1_conv_b_kx1": _L1_conv_in["b_kx1"],
        "L1_conv_w1": _L1_conv_in["w1"],
        "L1_conv_b1": _L1_conv_in["b1"],
    }

def reference(x, L0_conv_weight, L0_conv_bias, L0_conv_channel_mask, L0_conv_input_channel_mask, L1_conv_w_1xk, L1_conv_b_1xk, L1_conv_w_kx1, L1_conv_b_kx1, L1_conv_w1, L1_conv_b1):
    import jax
    import jax.numpy as jnp
    def _L0_conv_ref(x, weight, bias, channel_mask, input_channel_mask):
        import jax, jax.numpy as jnp
        import numpy as np

        def _masked_conv(x, weight, bias, channel_mask, input_channel_mask):
            w_eff = weight * channel_mask.astype(weight.dtype)[:, None, None, None] * input_channel_mask.astype(weight.dtype)[None, :, None, None]
            y = jax.lax.conv_general_dilated(x, w_eff, window_strides=(1, 1), padding=((1, 1), (1, 1)), rhs_dilation=(1, 1), dimension_numbers=('NCHW', 'OIHW', 'NCHW'))
            b_eff = bias * channel_mask.astype(bias.dtype)
            return y + b_eff[None, :, None, None]
        return _masked_conv(x, weight, bias, channel_mask, input_channel_mask)

    def _L1_conv_ref(x, w_1xk, b_1xk, w_kx1, b_kx1, w1, b1):
        import jax, jax.numpy as jnp
        import numpy as np
        B, C, H, W = (8, 64, 256, 256)
        SPLIT = 16
        K = 31
        PAD = K // 2
        DN = ('NCHW', 'OIHW', 'NCHW')

        def _dwconv(x, w, b, pad):
            y = jax.lax.conv_general_dilated(x, w, window_strides=(1, 1), padding=pad, dimension_numbers=DN, feature_group_count=w.shape[0])
            return y + b[None, :, None, None]
        x1, x2 = (x[:, :SPLIT], x[:, SPLIT:])
        x1 = _dwconv(x1, w_1xk, b_1xk, [(0, 0), (PAD, PAD)])
        x1 = _dwconv(x1, w_kx1, b_kx1, [(PAD, PAD), (0, 0)])
        out = jnp.concatenate((x1, x2), axis=1)
        out = jnp.einsum('bchw,oc->bohw', out, w1[:, :, 0, 0]) + b1[None, :, None, None]
        return jax.nn.gelu(out, approximate=False)

    def _gn(v, G=32, eps=1e-5):
        B_, C_, H_, W_ = v.shape
        g = v.reshape(B_, G, C_ // G, H_, W_)
        m = jnp.mean(g, axis=(2, 3, 4), keepdims=True)
        s = jnp.var(g, axis=(2, 3, 4), keepdims=True)
        return ((g - m) / jnp.sqrt(s + eps)).reshape(v.shape)

    def _ln_c(v, eps=1e-6):
        m = jnp.mean(v, axis=1, keepdims=True)
        s = jnp.var(v, axis=1, keepdims=True)
        return (v - m) / jnp.sqrt(s + eps)

    def _ln_t(v, eps=1e-5):
        m = jnp.mean(v, axis=-1, keepdims=True)
        s = jnp.var(v, axis=-1, keepdims=True)
        return (v - m) / jnp.sqrt(s + eps)

    def _to_tokens(v):
        B_, C_, H_, W_ = v.shape
        return v.reshape(B_, C_, H_ * W_).transpose(0, 2, 1)
    def _from_tokens(t, like):
        B_, C_, H_, W_ = like.shape
        return t.transpose(0, 2, 1).reshape(B_, C_, H_, W_)

    x = x + _L0_conv_ref(_gn(x), L0_conv_weight, L0_conv_bias, L0_conv_channel_mask, L0_conv_input_channel_mask)
    x = x + _L1_conv_ref(_gn(x), L1_conv_w_1xk, L1_conv_b_1xk, L1_conv_w_kx1, L1_conv_b_kx1, L1_conv_w1, L1_conv_b1)
    return x


_drawn_inputs = setup_inputs


def setup_inputs(seed=0):
    import zlib

    import numpy as np

    out = dict(_drawn_inputs(seed))
    spreads = {}
    factors = {'L0_conv_bias': 4.225,
     'L1_conv_w_1xk': 7.403,
     'L1_conv_b_1xk': 8.0,
     'L1_conv_w_kx1': 7.331,
     'L1_conv_b_kx1': 8.0}
    for name, (base, spread) in spreads.items():
        noise = np.random.default_rng([zlib.crc32(name.encode()), seed]).standard_normal(out[name].shape)
        drawn = base * np.exp(spread * noise) if base else spread * noise
        out[name] = jnp.asarray(drawn.astype(out[name].dtype))
    for name, factor in factors.items():
        out[name] = (out[name] * factor).astype(out[name].dtype)
    return out
```

```python
from contextlib import ExitStack

import concourse.bass as bass
from concourse import mybir

F32 = mybir.dt.float32
F16 = mybir.dt.float16
U8 = mybir.dt.uint8
ALU = mybir.AluOpType
ACT = mybir.ActivationFunctionType
AX = mybir.AxisListType

P = 128
PSUM_COLS = 512


def conv_preact_kernel(nc, x, w_co, w_ci, bias0, cmask, imask, k_v, k_h, b_h, b_v, w1t, b1,
                       ident, group_avg, pick, x1_sel, out):
    NI, C, H, W = x.shape
    NB = H // 2
    BL = 4
    CH = NB // BL
    UN = 4
    TI = CH // UN
    SPLIT = k_v.shape[0]
    K = k_v.shape[1]
    PAD = K // 2
    HH = H // 2
    BAND = HH + PAD
    TW = BAND + PAD
    ZW = W + 2
    N = 2 * W
    ZS = 64.0
    WS = 512.0
    assert CH * BL == NB and TI * UN == CH and HH == NB and 2 * C == P and H == W and UN == 4

    rows = "c (b two) w -> two c b w"
    s_dram = nc.dram_tensor("s_x1_split", (SPLIT, NB + 1, 2, W), F32, kind="Internal").ap()
    d_dram = nc.dram_tensor("s_dw_out", (SPLIT, H, W), F32, kind="Internal").ap()
    skew = nc.dram_tensor("s_taps", (2 * SPLIT, HH, 2 * P + 1), F32, kind="Internal")
    s_rows = s_dram.rearrange("c b two w -> c (b two) w")
    d_blocks = d_dram.rearrange(rows, two=2)

    with ExitStack() as ctx:
        def sb(name, shape, dt=F32):
            return ctx.enter_context(nc.sbuf_tensor(name, shape, dt))

        def sem(name):
            return ctx.enter_context(nc.semaphore(name))

        x1 = sb("x1", [P, NB + 1, W])
        xt = sb("xt", [P, 4, BL + 1, W])
        z32 = sb("z32", [P, 2, BL, W])
        zh = sb("zh", [P, 2, BL + 1, ZW], F16)
        zl = sb("zl", [P, 2, BL + 1, ZW], F16)
        xs = sb("xs", [P, 2, BL, W])
        gt = sb("gt", [P, 4, BL, W])
        toe = sb("toe", [HH, 2 * SPLIT, TW])
        zt = sb("zt", [HH, 4, 2, W])
        pa = sb("pa", [HH, 2, 2, W])
        dt_ = sb("dwt", [HH, 4, 2, W])
        wt = sb("wt", [P, 2, 2, 3, P], F16)
        w1bd = sb("w1bd", [P, P])
        w1n = sb("w1n", [P, P])
        gavg = sb("gavg", [P, P])
        ones = sb("ones", [P, P])
        pick_sb = sb("pick_sb", [P, SPLIT])
        sel = sb("sel", [P, 2])
        st1 = sb("st1", [P, 2 * CH, 6])
        st2 = sb("st2", [P, 2 * CH, 6])
        mv = sb("mv", [P, 2, 2])
        v = sb("v", [P, 40])
        bcin = sb("bcin", [P, 2 * SPLIT])
        bc = sb("bc", [P, 2 * SPLIT])
        dbias = sb("dbias", [HH, SPLIT, 2])
        m8 = sb("m8", [P, 2], U8)
        bhv = sb("bhv", [1, 2, SPLIT])
        zrow = sb("zrow", [P, ZW], F16)
        ps = ctx.enter_context(nc.psum_tensor("ps", [P, 8, PSUM_COLS], F32))

        def col(k):
            return v[:, k:k + 1]

        (B0, B1, SOUT, MINV, MAXV, AMAX, RAMAX, CM, IM, M1, R1, NB1, RS2, SH2, BU, T0, T1,
         PW, _, GATE) = range(19 + 1)
        M, DM, SQ, VE, R0, NT = (slice(20 + 2 * k, 22 + 2 * k) for k in range(6))

        wco_sb = x1[:, 1:4, :].rearrange("p a b -> p (a b)")[:, 0:9 * C]
        wci_sb = x1[:, 4:7, :].rearrange("p a b -> p (a b)")[:, 0:9 * C].rearrange("p (t c) -> p t c", c=C)
        wsc = x1[:, 7:10, :].rearrange("p a b -> p (a b)")[:, 0:9 * C].rearrange("p (t c) -> p t c", c=C)
        rb = x1[:, 10, 0:C]
        idn = x1[0:C, 11, 0:C]
        dia = x1[0:C, 12, 0:C]
        wlo = x1[:, 13:16, :].rearrange("p a b -> p (a b)")[:, 0:9 * C].rearrange("p (t c) -> p t c", c=C)
        taps = x1[0:2 * SPLIT, 20:22, :].rearrange("p a b -> p (a b)")[:, 0:2 * P]
        vsum = x1[0:HH, 24:24 + SPLIT, :]
        whi = zh[:, 0, :, :].rearrange("p a b -> p (a b)")[:, 0:9 * C].rearrange("p (t c) -> p t c", c=C)

        params_in, taps_in, taps_out, toe_in = map(sem, ("params_in", "taps_in", "taps_out", "toe_in"))
        prep = sem("prep")
        prep_pe = sem("prep_pe")
        x_in = [sem(f"x_in{k}") for k in range(4)]
        s_in = [sem(f"s_in{k}") for k in range(2)]
        stat_used = sem("stat_used")
        z32_done, zh_done, zl_done, halo_done = map(sem, ("z32_done", "zh_done", "zl_done", "halo_done"))
        conv_done, evac_done, saved = map(sem, ("conv_done", "evac_done", "saved"))
        gn_step, gn_mm, gn_pow = map(sem, ("gn_step", "gn_mm", "gn_pow"))
        gn_sq, st2_done = sem("gn_sq"), sem("st2_done")
        zt_in = [sem(f"zt_in{k}") for k in range(4)]
        znorm, va_done, pa_done, vb_done, dw_done = map(
            sem, ("znorm", "va_done", "pa_done", "vb_done", "dw_done"))
        d_out = [sem(f"d_out{k}") for k in range(4)]
        d_in = [sem(f"d_in{k}") for k in range(4)]
        r_in = [sem(f"r_in{k}") for k in range(4)]
        mix_done, gelu_done, sum_done = map(sem, ("mix_done", "gelu_done", "sum_done"))
        o_out = [sem(f"o_out{k}") for k in range(4)]

        GN_STEPS, GN_MMS = 17, 4
        FIRST_STEPS, FIRST_MMS = 11, 2
        LAST = NI - 1

        block = ctx.enter_context(nc.Block())

        def chunks(eng, n, step, first_static, last_static):
            a, b = int(first_static), TI - int(last_static)
            if first_static:
                for u in range(UN):
                    step(0, u)
            with eng.Fori(a, b) as t:
                for u in range(UN):
                    step(t, u)
            if last_static:
                for u in range(UN):
                    step(TI - 1, u)

        def images(eng, image):
            with eng.Fori(0, LAST) as n:
                image(n, False)
            image(LAST, True)

        @block.sync
        def _(sp):
            def load_stats(n, g, t, u):
                xb = x[n].rearrange(rows, two=2)
                sp.wait_ge(stat_used, g * CH + UN * t + u + 1)
                for par in range(2):
                    sp.dma_start(xs[64 * par:64 * par + 64, u % 2], xb[par][:, bass.ds((UN * t + u) * BL, BL), :]
                                 ).then_inc(s_in[u % 2], 16)

            def load_x(n, t, u):
                xb = x[n].rearrange(rows, two=2)
                sp.dma_start(xt[0:64, u, 1:BL + 1], xb[0][:, bass.ds((UN * t + u) * BL, BL), :]
                             ).then_inc(x_in[u], 16)
                if isinstance(t, int) and t == 0 and u == 0:
                    sp.dma_start(xt[64:128, u, 1:BL + 1], xb[1][:, 0:BL, :]).then_inc(x_in[u], 16)
                else:
                    sp.dma_start(xt[64:128, u, :], xb[1][:, bass.ds((UN * t + u) * BL - 1, BL + 1), :]
                                 ).then_inc(x_in[u], 16)

            def save(n, t, u):
                i = UN * t + u
                sp.wait_ge(evac_done, n * CH + i + 2)
                sp.dma_start(s_dram[:, bass.ds(i * BL + 1, BL), 0, :], x1[0:SPLIT, bass.ds(i * BL + 1, BL), :]
                             ).then_inc(saved, 16)
                k = BL + (isinstance(i, int) and i == CH - 1)
                sp.dma_start(s_dram[:, bass.ds(i * BL, k), 1, :], x1[64:64 + SPLIT, bass.ds(i * BL, k), :]
                             ).then_inc(saved, 16)

            for par in range(2):
                h = slice(64 * par, 64 * par + 64)
                masks = [m.bitcast(U8).rearrange("a c -> c a") for m in (cmask, imask)]
                for dst, src in ((wco_sb[h], w_co), (wci_sb[h], w_ci), (v[h, B0:B0 + 1], bias0),
                                 (v[h, B1:B1 + 1], b1), (m8[h, 0:1], masks[0]), (m8[h, 1:2], masks[1])):
                    sp.dma_start(dst, src).then_inc(params_in, 16)
            sp.dma_start(idn, ident).then_inc(params_in, 16)
            sp.dma_start(gavg[:], group_avg).then_inc(params_in, 16)
            sp.dma_start(pick_sb[:], pick).then_inc(params_in, 16)
            sp.dma_start(sel[:], x1_sel).then_inc(params_in, 16)
            sp.dma_start(bhv[:, 0, :], b_h).then_inc(params_in, 16)
            sp.dma_start(bhv[:, 1, :], b_v).then_inc(params_in, 16)
            sp.wait_ge(prep, 1)
            off = HH - 1
            sp.dma_start(taps[0:SPLIT, off:off + K], k_v).then_inc(taps_in, 16)
            sp.dma_start(taps[SPLIT:2 * SPLIT, off:off + K], k_h).then_inc(taps_in, 16)
            sp.dma_start(w1bd[0:64, 0:64], w1t).then_inc(taps_in, 16)
            sp.dma_start(w1bd[64:128, 64:128], w1t).then_inc(taps_in, 16)
            sp.wait_ge(taps_in, 64)
            sp.dma_start(skew.ap()[:, :, 0:2 * P],
                         taps.rearrange("f (a k) -> f a k", a=1).broadcast_to([2 * SPLIT, HH, 2 * P])
                         ).then_inc(taps_out, 16)
            sp.wait_ge(taps_out, 16)
            sp.dma_start(toe[:], bass.AP(skew, off, [[2 * P, HH], [HH * (2 * P + 1), 2 * SPLIT], [1, TW]])
                         ).then_inc(toe_in, 16)
            chunks(sp, 0, lambda t, u: load_stats(0, 0, t, u), False, False)
            for u in range(UN):
                load_x(0, 0, u)

            def image(n, last):
                def conv_step(t, u):
                    if not (isinstance(t, int) and t == 0):
                        save(n, t - 1, u)
                        load_x(n, t, u)
                    if not last:
                        load_stats(n + 1, n + 1, t, u)

                chunks(sp, n, conv_step, True, False)
                for u in range(UN):
                    save(n, TI - 1, u)
                if not last:
                    for u in range(UN):
                        load_x(n + 1, 0, u)
                sp.wait_ge(saved, (n + 1) * 32 * CH)

                def load_plane(c, u):
                    sp.dma_start(zt[:, u], s_rows[bass.ds(c, 1), 2:2 + H, :].rearrange("a (m p) w -> p (a m) w", m=2)
                                 ).then_inc(zt_in[u], 16)

                def store_plane(c, u):
                    sp.wait_ge(dw_done, n * SPLIT + c + 2)
                    sp.dma_start(d_dram[bass.ds(c, 1)].rearrange("a (m p) w -> p (a m) w", m=2), dt_[:, u]
                                 ).then_inc(d_out[u], 16)

                for u in range(4):
                    load_plane(u, u)
                with sp.Fori(0, SPLIT // 4 - 1) as q:
                    for u in range(4):
                        store_plane(4 * q + u, u)
                        load_plane(4 * q + u + 4, u)
                for u in range(4):
                    store_plane(SPLIT - 4 + u, u)
                for u in range(4):
                    sp.wait_ge(d_out[u], (n + 1) * 16 * (SPLIT // 4))

                def to_x1(src_even, src_odd, i, s):
                    sp.dma_start(x1[0:SPLIT, bass.ds(i * BL + 1, BL), :], src_even).then_inc(s, 16)
                    sp.dma_start(x1[64:64 + SPLIT, bass.ds(i * BL + 1, BL), :], src_odd).then_inc(s, 16)

                def load_d(t, u):
                    i = UN * t + u
                    b = bass.ds(i * BL, BL)
                    to_x1(d_blocks[0][:, b, :], d_blocks[1][:, b, :], i, d_in[u])

                def mix_step(t, u):
                    i = UN * t + u
                    sp.wait_ge(mix_done, n * CH + i + 1)
                    b = bass.ds(i * BL + 1, BL)
                    to_x1(s_dram[:, b, 0, :], s_dram[:, b, 1, :], i, r_in[u])
                    if not (isinstance(t, int) and t == TI - 1):
                        load_d(t + 1, u)

                for u in range(UN):
                    load_d(0, u)
                chunks(sp, n, mix_step, False, True)

            images(sp, image)
            for k in range(4):
                sp.wait_ge(o_out[k], 32 * TI * NI)

        @block.gpsimd
        def _(pool):
            def power(k, cols):
                pool.wait_ge(gn_step, k)
                nc.gpsimd.tensor_tensor(v[:, R0][:, cols], v[:, VE][:, cols], v[:, PW:PW + 2][:, cols], ALU.pow
                                        ).then_inc(gn_pow, 1)

            power(5, slice(0, 1))

            def image(n, last):
                power(FIRST_STEPS + n * GN_STEPS + 5, slice(1, 2) if last else slice(0, 2))

            images(pool, image)

        def z_waits(eng, n, t, u):
            j = UN * t + u
            first = isinstance(t, int) and j == 0
            eng.wait_ge(x_in[u], 32 * (TI * n + t + 1))
            eng.wait_ge(conv_done, n * CH + (0 if first else j - 1))
            eng.wait_ge(halo_done, n * CH + j)

        @block.scalar
        def _(act):
            def z_high(n, t, u):
                z_waits(act, n, t, u)
                nc.scalar.activation(zh[:, u % 2, 1:BL + 1, 1:W + 1], xt[:, u, 1:BL + 1, :], ACT.Identity,
                                     bias=col(NB1), scale=col(R1)).then_inc(zh_done, 1)

            def halo(n, t, u):
                j = UN * t + u
                act.wait_ge(zl_done, n * CH + j + 1)
                act.wait_ge(zh_done, n * CH + j + 1)
                act.wait_ge(conv_done, n * CH + j)
                a, b = u % 2, (u + 1) % 2
                nc.scalar.copy(zh[:, b, 0, :], zh[:, a, BL, :])
                nc.scalar.copy(zl[:, b, 0, :], zl[:, a, BL, :]).then_inc(halo_done, 1)

            act.wait_ge(halo_done, 1)
            act.wait_ge(gn_step, FIRST_STEPS)
            z_high(0, 0, 0)

            def image(n, last):
                def conv_step(t, u):
                    halo(n, t, u)
                    z_high(n, t + (u + 1) // UN, (u + 1) % UN)

                with act.Fori(0, TI - 1) as t:
                    for u in range(UN):
                        conv_step(t, u)
                for u in range(UN - 1):
                    conv_step(TI - 1, u)
                act.wait_ge(conv_done, n * CH + CH - 1)
                nc.scalar.copy(zh[:, 0, 0, :], zrow[:, :])
                nc.scalar.copy(zl[:, 0, 0, :], zrow[:, :]).then_inc(halo_done, 1)

                act.wait_ge(gn_step, FIRST_STEPS + (n + 1) * GN_STEPS)
                if not last:
                    z_high(n + 1, 0, 0)

                def plane_norm(q, u):
                    c = 4 * q + u
                    act.wait_ge(zt_in[u], 16 * ((SPLIT // 4) * n + q + 1))
                    nc.scalar.activation(zt[:, u], zt[:, u], ACT.Identity, bias=bc[0:HH, bass.ds(c + SPLIT, 1)],
                                         scale=bc[0:HH, bass.ds(c, 1)]).then_inc(znorm, 1)

                def plane_out(q, u):
                    c = 4 * q + u
                    act.wait_ge(vb_done, n * SPLIT + c + 1)
                    act.wait_ge(d_out[u], 16 * ((SPLIT // 4) * n + q))
                    for m in range(2):
                        ins = nc.scalar.activation(
                            dt_[:, u, m, :], ps[0:HH, u % 2, m * W:(m + 1) * W], ACT.Identity,
                            bias=dbias[:, bass.ds(c, 1), m], scale=1.0)
                    ins.then_inc(dw_done, 1)

                plane_norm(0, 0)
                plane_norm(0, 1)
                with act.Fori(0, SPLIT // 4 - 1) as q:
                    for u in range(4):
                        plane_norm(q + (u + 2) // 4, (u + 2) % 4)
                        plane_out(q, u)
                for u in range(4):
                    if u < 2:
                        plane_norm(SPLIT // 4 - 1, u + 2)
                    plane_out(SPLIT // 4 - 1, u)

                ob = out[n].rearrange(rows, two=2)

                def store(t, u):
                    i = UN * t + u
                    act.wait_ge(sum_done, n * CH + i + 1)
                    for par in range(2):
                        act.dma_start(ob[par][:, bass.ds(i * BL, BL), :], gt[64 * par:64 * par + 64, u]
                                      ).then_inc(o_out[u], 16)

                def gelu_step(t, u):
                    i = UN * t + u
                    act.wait_ge(mix_done, n * CH + i + 1)
                    act.wait_ge(o_out[u], 32 * (TI * n + t))
                    b = 2 + 2 * (u % 2)
                    nc.scalar.activation(gt[:, u].rearrange("p (g r) w -> p g (r w)", g=2), ps[:, b:b + 2, 0:N],
                                         ACT.Gelu, bias=col(BU), scale=1.0).then_inc(gelu_done, 1)
                    if u >= 2:
                        store(t, u - 2)
                    elif not (isinstance(t, int) and t == 0):
                        store(t - 1, u + 2)

                chunks(act, n, gelu_step, True, False)
                store(TI - 1, 2)
                store(TI - 1, 3)

            images(act, image)

        @block.tensor
        def _(pe):
            pe.wait_ge(prep, 8)
            nc.tensor.matmul(ps[:, 7, 0:C], ones[0:C, :], dia, start=True, stop=True).then_inc(prep_pe, 1)
            pe.wait_ge(toe_in, 16)
            for c in range(SPLIT):
                if c >= 2:
                    pe.wait_ge(prep, 12 + c - 1)
                o = ps[0:HH, c % 2, :]
                nc.tensor.matmul(o[:, 0:BAND], ones[0:HH, 0:HH], toe[:, c, PAD:TW], start=True, stop=False,
                                 skip_group_check=True)
                nc.tensor.matmul(o[:, H - BAND:H], ones[0:HH, 0:HH], toe[:, c, 0:BAND], start=False, stop=True,
                                 skip_group_check=True).then_inc(prep_pe, 1)
            for c in range(SPLIT):
                pe.wait_ge(prep, 12 + c + 1)
                for m in range(2):
                    o = ps[0:HH, 4, 2 * c + m:2 * c + m + 1]
                    nc.tensor.matmul(o, vsum[0:1, c, m * HH:(m + 1) * HH], bhv[:, 0, c:c + 1],
                                     start=True, stop=False)
                    ins = nc.tensor.matmul(o, ones[0:1, 0:HH], bhv[:, 1, c:c + 1], start=False, stop=True)
            ins.then_inc(prep_pe, 1)

            def gn(steps, mms, cols, layer1):
                k = slice(0, 2) if cols == 2 else slice(cols, cols + 1)
                pe.wait_ge(gn_step, steps + 2)
                nc.tensor.matmul(ps[:, 7, 0:2][:, k], gavg[:], mv[:, k, 0], start=True, stop=True).then_inc(gn_mm, 1)
                pe.wait_ge(gn_step, steps + 4)
                nc.tensor.matmul(ps[:, 7, 2:4][:, k], gavg[:], v[:, VE][:, k], start=True, stop=True
                                 ).then_inc(gn_mm, 1)
                if layer1:
                    pe.wait_ge(gn_step, steps + 15)
                    nc.tensor.matmul(ps[:, 7, 4:5], w1bd[:], col(SH2), start=True, stop=True).then_inc(gn_mm, 1)
                    nc.tensor.matmul(ps[:, 7, 8:8 + 2 * SPLIT], ones[:], bcin[:], start=True, stop=True
                                     ).then_inc(gn_mm, 1)

            gn(0, 0, 0, False)

            def image(n, last):
                def conv(t, u):
                    j = UN * t + u
                    pe.wait_ge(zh_done, n * CH + j + 1)
                    pe.wait_ge(zl_done, n * CH + j + 1)
                    pe.wait_ge(halo_done, n * CH + j + 1)
                    pe.wait_ge(gelu_done, n * CH)
                    pe.wait_ge(evac_done, n * CH + j)
                    z = u % 2
                    terms = [(hl, zz, a, kx) for hl, zz in ((0, zh), (0, zl), (1, zh))
                             for a in range(2) for kx in range(3)]
                    for k, (hl, zz, a, kx) in enumerate(terms):
                        for g in range(2):
                            ins = nc.tensor.matmul(ps[:, 2 * z + g, 0:N], wt[:, hl, a, kx, :],
                                                   zz[:, z, 2 * g + a:2 * g + a + 2, kx:kx + W],
                                                   start=(k == 0), stop=(k == len(terms) - 1))
                    if isinstance(t, int) and j == CH - 1:
                        terms = [q for q in terms if q[2] == 0]
                        for k, (hl, zz, a, kx) in enumerate(terms):
                            ins = nc.tensor.matmul(ps[:, 6, 0:W], wt[:, hl, 0, kx, :], zz[:, z, BL, kx:kx + W],
                                                   start=(k == 0), stop=(k == len(terms) - 1))
                    ins.then_inc(conv_done, 1)

                chunks(pe, n, conv, False, True)
                gn(FIRST_STEPS + n * GN_STEPS, 0, 1 if last else 2, True)

                def vertical(q, u):
                    c = 4 * q + u
                    pe.wait_ge(znorm, n * SPLIT + c + 1)
                    pe.wait_ge(pa_done, n * SPLIT + c)
                    o = ps[0:HH, 4 + u % 2, :]
                    tv = toe[:, bass.ds(c, 1), :]
                    for m in range(2):
                        lhs = [zt[:, u, k, m * HH:(m + 1) * HH] for k in range(2)]
                        nc.tensor.matmul(o[:, m * H:m * H + BAND], lhs[0], tv[:, 0, PAD:TW],
                                         start=(m == 0), stop=False, skip_group_check=True)
                        ins = nc.tensor.matmul(o[:, m * H + H - BAND:m * H + H], lhs[1], tv[:, 0, 0:BAND],
                                               start=False, stop=(m == 1), skip_group_check=True)
                    ins.then_inc(va_done, 1)

                def horizontal(q, u):
                    c = 4 * q + u
                    pe.wait_ge(pa_done, n * SPLIT + c + 2)
                    pe.wait_ge(dw_done, n * SPLIT + c)
                    o = ps[0:HH, u % 2, :]
                    th = toe[:, bass.ds(c + SPLIT, 1), :]
                    for m in range(2):
                        lhs = [pa[:, u % 2, k, m * HH:(m + 1) * HH] for k in range(2)]
                        nc.tensor.matmul(o[:, m * W:m * W + BAND], lhs[0], th[:, 0, PAD:TW],
                                         start=(m == 0), stop=False, skip_group_check=True)
                        ins = nc.tensor.matmul(o[:, m * W + W - BAND:m * W + W], lhs[1], th[:, 0, 0:BAND],
                                               start=False, stop=(m == 1), skip_group_check=True)
                    ins.then_inc(vb_done, 1)

                vertical(0, 0)
                with pe.Fori(0, SPLIT // 4 - 1) as q:
                    for u in range(4):
                        vertical(q + (u + 1) // 4, (u + 1) % 4)
                        horizontal(q, u)
                for u in range(4):
                    if u < 3:
                        vertical(SPLIT // 4 - 1, u + 1)
                    horizontal(SPLIT // 4 - 1, u)

                def mix(t, u):
                    i = UN * t + u
                    pe.wait_ge(d_in[u], 32 * (TI * n + t + 1))
                    if u >= 2 or not isinstance(t, int) or t > 0:
                        pe.wait_ge(gelu_done, n * CH + i - 1 if not (isinstance(t, int) and t == 0) else n * CH + u - 1)
                    for g in range(2):
                        ins = nc.tensor.matmul(ps[:, 2 + 2 * (u % 2) + g, 0:N], w1n[:],
                                               x1[:, bass.ds(i * BL + 1 + 2 * g, 2), :], start=True, stop=True)
                    ins.then_inc(mix_done, 1)

                chunks(pe, n, mix, True, False)

            images(pe, image)

        @block.vector
        def _(dve):
            dve_ = nc.vector

            def step(ins):
                at[0] += 1
                ins.then_inc(prep, 1)
                dve.wait_ge(prep, at[0])

            at = [0]
            dve_.memset(w1bd[:], 0.0).then_inc(evac_done, 1)
            dve_.memset(ones[:], 1.0).then_inc(stat_used, 2)
            dve_.memset(v[:, PW:PW + 2], -0.5).then_inc(pa_done, 1)
            dve_.memset(v[:, T0:T0 + 1], 0.0).then_inc(dw_done, 1)
            dve_.memset(x1[:, 0, :], 0.0)
            dve_.memset(xt[64:128, 0, 0, :], 0.0)
            dve_.memset(zl[:], 0.0)
            step(dve_.memset(taps, 0.0))
            dve.wait_ge(params_in, 16 * 18)
            dve_.tensor_reduce(col(MAXV), wco_sb, AX.X, ALU.max)
            dve_.tensor_copy(v[:, CM:CM + 2], m8[:])
            step(dve_.tensor_reduce(col(MINV), wco_sb, AX.X, ALU.min))
            step(dve_.tensor_scalar(col(MINV), col(MINV), -1.0, 1e-30, ALU.mult, ALU.max))
            step(dve_.tensor_tensor(col(AMAX), col(MAXV), col(MINV), ALU.max))
            dve_.tensor_scalar(col(SOUT), col(AMAX), 1.0 / (WS * ZS), None, ALU.mult)
            step(dve_.reciprocal(col(RAMAX), col(AMAX)))
            step(dve_.tensor_scalar(col(RAMAX), col(RAMAX), col(CM), WS, ALU.mult, ALU.mult))
            dve_.tensor_scalar(col(B0), col(B0), col(CM), None, ALU.mult)
            step(dve_.tensor_scalar(dia, idn, v[0:C, RAMAX:RAMAX + 1], None, ALU.mult))
            step(dve_.tensor_scalar(wsc, wci_sb, col(IM), None, ALU.mult))
            dve.wait_ge(prep_pe, 1)
            step(dve_.tensor_copy(rb, ps[:, 7, 0:C]))
            step(dve_.tensor_tensor(wsc, wsc, rb.rearrange("p (a c) -> p a c", a=1).broadcast_to([P, 9, C]), ALU.mult))
            step(dve_.tensor_copy(whi, wsc))
            step(dve_.tensor_tensor(wlo, wsc, whi, ALU.subtract))
            assert at[0] == 12, at
            for c in range(SPLIT):
                dve.wait_ge(prep_pe, 2 + c)
                step(dve_.tensor_copy(vsum[:, c, :], ps[0:HH, c % 2, 0:H]))
            step(dve_.memset(wt[:], 0.0))
            taps_of = {(0, 0): (None, 0), (0, 1): (0, 1), (1, 0): (1, 2), (1, 1): (2, None)}
            for (a, par_in), kys in taps_of.items():
                h = slice(64 * par_in, 64 * par_in + 64)
                for m, ky in enumerate(kys):
                    if ky is not None:
                        dve_.tensor_copy(wt[h, 0, a, :, 64 * m:64 * m + 64], whi[h, 3 * ky:3 * ky + 3, :])
                        ins = dve_.tensor_copy(wt[h, 1, a, :, 64 * m:64 * m + 64], wlo[h, 3 * ky:3 * ky + 3, :])
            step(ins)
            dve.wait_ge(prep_pe, 2 + SPLIT)
            step(dve_.memset(zrow[:], 0.0))
            dve_.tensor_copy(dbias[:].rearrange("p c m -> p (c m)"), ps[0:HH, 4, 0:2 * SPLIT])
            dve_.memset(zh[:], 0.0).then_inc(halo_done, 1)
            dve.wait_ge(halo_done, 1)

            def chunk_stats(g, t, u):
                i = UN * t + u
                dve.wait_ge(s_in[u % 2], 32 * ((CH // 2) * g + 2 * t + u // 2 + 1))
                for r in range(2):
                    ins = dve_.bn_stats(st1[:, bass.ds(2 * i + r, 1), :].rearrange("p a s -> p (a s)"),
                                        xs[:, u % 2, 2 * r:2 * r + 2, :])
                ins.then_inc(stat_used, 1)

            def gn(base, stats, cols, layer1):
                k = slice(0, 2) if cols == 2 else slice(cols, cols + 1)
                done = [0]
                mm = base[1]

                def link(ins, count=1):
                    done[0] += 1
                    ins.then_inc(gn_step, 1)
                    dve.wait_ge(gn_step, base[0] + done[0])

                dve_.memset(col(GATE), 0.0)
                if cols in (0, 2):
                    ins = dve_.bn_aggr(mv[:, 0, :], st1[:])
                if cols in (1, 2):
                    ins = dve_.bn_aggr(mv[:, 1, :], st2[:])
                link(ins)
                link(dve_.tensor_tensor(mv[:, 1, 0:1], mv[:, 1, 0:1], col(B0), ALU.add) if layer1
                     else dve_.memset(v[:, T0:T0 + 1], 0.0))
                dve.wait_ge(gn_mm, mm + 1)
                dve_.tensor_copy(v[:, M][:, k], ps[:, 7, 0:2][:, k])
                link(dve_.tensor_tensor(v[:, DM][:, k], mv[:, k, 0], ps[:, 7, 0:2][:, k], ALU.subtract))
                dve_.tensor_tensor(v[:, SQ][:, k], v[:, DM][:, k], v[:, DM][:, k], ALU.mult).then_inc(gn_sq, 1)
                dve.wait_ge(gn_sq, base[2] + 1)
                link(dve_.tensor_tensor(v[:, VE][:, k], mv[:, k, 1], v[:, SQ][:, k], ALU.add))
                dve.wait_ge(gn_mm, mm + 2)
                link(dve_.tensor_scalar(v[:, VE][:, k], ps[:, 7, 2:4][:, k], 1e-5, None, ALU.add))
                dve.wait_ge(gn_pow, base[2] + 1)
                link(dve_.tensor_tensor(v[:, NT][:, k], v[:, R0][:, k], v[:, R0][:, k], ALU.mult))
                link(dve_.tensor_tensor(v[:, NT][:, k], v[:, NT][:, k], v[:, VE][:, k], ALU.mult))
                link(dve_.tensor_scalar(v[:, NT][:, k], v[:, NT][:, k], -0.5, 1.5, ALU.mult, ALU.add))
                link(dve_.tensor_tensor(v[:, R0][:, k], v[:, R0][:, k], v[:, NT][:, k], ALU.mult))
                if cols in (0, 2):
                    dve_.tensor_copy(col(M1), v[:, 20:21])
                    link(dve_.tensor_scalar(col(R1), v[:, 28:29], ZS, None, ALU.mult))
                    link(dve_.scalar_tensor_tensor(col(NB1), v[:, 20:21], -1.0, col(R1), ALU.mult, ALU.mult))
                elif layer1:
                    for _ in range(2):
                        link(dve_.memset(v[:, T0:T0 + 1], 0.0))
                if layer1:
                    r2, m2 = v[:, 29:30], v[:, 21:22]
                    link(dve_.tensor_tensor(col(T0), col(B0), m2, ALU.subtract))
                    link(dve_.tensor_tensor(col(T1), col(T0), r2, ALU.mult))
                    dve_.tensor_scalar(bcin[:, 0:SPLIT], pick_sb[:], r2, None, ALU.mult)
                    dve_.tensor_scalar(bcin[:, SPLIT:2 * SPLIT], pick_sb[:], col(T1), None, ALU.mult)
                    dve_.tensor_tensor(col(SH2), col(T1), sel[:, 1:2], ALU.mult)
                    link(dve_.scalar_tensor_tensor(col(RS2), r2, sel[:, 1:2], sel[:, 0:1], ALU.mult, ALU.add))
                    link(dve_.tensor_scalar(w1n[:], w1bd[:], col(RS2), None, ALU.mult))
                    dve.wait_ge(gn_mm, mm + 4)
                    dve_.tensor_tensor(col(BU), ps[:, 7, 4:5], col(B1), ALU.add)
                    link(dve_.tensor_copy(bc[:], ps[:, 7, 8:8 + 2 * SPLIT]))
                    link(dve_.memset(v[:, T0:T0 + 1], 0.0))
                assert done[0] == (GN_STEPS if layer1 else FIRST_STEPS), done

            def z_low(n, t, u):
                j = UN * t + u
                first = isinstance(t, int) and j == 0
                z_waits(dve, n, t, u)
                dve.wait_ge(zl_done, n * CH + (0 if first else j - 1))
                dve_.tensor_scalar(z32[:, u % 2], xt[:, u, 1:BL + 1, :], col(M1), col(R1), ALU.subtract, ALU.mult
                                   ).then_inc(z32_done, 1)
                dve.wait_ge(z32_done, n * CH + j + 1)
                dve.wait_ge(zh_done, n * CH + j + 1)
                dve_.tensor_tensor(zl[:, u % 2, 1:BL + 1, 1:W + 1], z32[:, u % 2],
                                   zh[:, u % 2, 1:BL + 1, 1:W + 1], ALU.subtract).then_inc(zl_done, 1)

            chunks(dve, 0, lambda t, u: chunk_stats(0, t, u), False, False)
            dve.wait_ge(stat_used, 2 + CH)
            gn((0, 0, 0), st1, 0, False)
            z_low(0, 0, 0)

            def image(n, last):
                def conv_out(t, u):
                    j = UN * t + u
                    tail = isinstance(t, int) and j == CH - 1
                    dve.wait_ge(sum_done, n * CH)
                    dve.wait_ge(conv_done, n * CH + j + 1)
                    s = slice(0, 64), slice(64, 128)
                    for g in range(2):
                        for par in range(2):
                            h = s[par]
                            a = 2 * g + 1 - par
                            ins = dve_.scalar_tensor_tensor(
                                x1[h, bass.ds(j * BL + a, 2), :],
                                ps[h, 2 * (u % 2) + g, 0:N].rearrange("p (r w) -> p r w", r=2),
                                v[h, SOUT:SOUT + 1], xt[h, u, a:a + 2, :], ALU.mult, ALU.add)
                    if tail:
                        ins = dve_.scalar_tensor_tensor(x1[s[1], NB, :], ps[s[1], 6, 0:W], v[s[1], SOUT:SOUT + 1],
                                                        xt[s[1], u, BL, :], ALU.mult, ALU.add)
                    ins.then_inc(evac_done, 1)
                    dve.wait_ge(evac_done, n * CH + j + 2)
                    for r in range(2):
                        ins = dve_.bn_stats(st2[:, bass.ds(2 * j + r, 1), :].rearrange("p a s -> p (a s)"),
                                            x1[:, bass.ds(j * BL + 2 * r, 2), :])
                    if tail:
                        ins.then_inc(st2_done, 1)
                        dve.wait_ge(st2_done, 2 * n + 1)
                        dve_.bn_stats(st2[:, 0, :], x1[:, 1:NB + 1:NB - 1, :]).then_inc(st2_done, 1)
                        dve.wait_ge(st2_done, 2 * n + 2)

                def conv_step(t, u):
                    if not (isinstance(t, int) and UN * t + u == CH - 1):
                        z_low(n, t + (u + 1) // UN, (u + 1) % UN)
                    conv_out(t, u)
                    if not last:
                        chunk_stats(n + 1, t, u)

                chunks(dve, n, conv_step, False, True)
                if not last:
                    dve.wait_ge(stat_used, 2 + (n + 2) * CH)
                gn((FIRST_STEPS + n * GN_STEPS, FIRST_MMS + n * GN_MMS, n + 1), None, 1 if last else 2, True)
                if not last:
                    z_low(n + 1, 0, 0)

                def plane_turn(q, u):
                    c = 4 * q + u
                    dve.wait_ge(va_done, n * SPLIT + c + 1)
                    first = isinstance(q, int) and q == 0 and u == 0
                    dve.wait_ge(vb_done, n * SPLIT + (0 if first else c - 1))
                    dve_.tensor_copy(pa[:, u % 2].rearrange("p m w -> p (m w)"), ps[0:HH, 4 + u % 2, 0:N]
                                     ).then_inc(pa_done, 1)

                for u in range(4):
                    plane_turn(0, u)
                with dve.Fori(1, SPLIT // 4) as q:
                    for u in range(4):
                        plane_turn(q, u)

                def add(t, u):
                    i = UN * t + u
                    dve.wait_ge(gelu_done, n * CH + i + 1)
                    dve.wait_ge(r_in[u], 32 * (TI * n + t + 1))
                    dve_.scalar_tensor_tensor(gt[:, u], gt[:, u], col(B0), x1[:, bass.ds(i * BL + 1, BL), :],
                                              ALU.add, ALU.add).then_inc(sum_done, 1)

                chunks(dve, n, add, False, False)

            images(dve, image)


def kernel(**inputs):
    import numpy as _np
    import concourse.bacc as _bacc
    from concourse.bass_utils import run_bass_kernel_spmd as _run

    x = _np.ascontiguousarray(inputs["x"])
    w = _np.asarray(inputs["L0_conv_weight"])
    C = w.shape[0]
    split, taps = inputs["L1_conv_w_1xk"].shape[0], inputs["L1_conv_w_1xk"].shape[3]
    ch = _np.arange(2 * C) % C
    sel = (ch < split)
    arrays = {
        "x": x,
        "w_co": w.reshape(C, -1),
        "w_ci": w.transpose(1, 2, 3, 0).reshape(C, -1, C),
        "bias0": inputs["L0_conv_bias"].reshape(C, 1),
        "cmask": _np.asarray(inputs["L0_conv_channel_mask"]).view(_np.int32).reshape(1, -1),
        "imask": _np.asarray(inputs["L0_conv_input_channel_mask"]).view(_np.int32).reshape(1, -1),
        "k_v": inputs["L1_conv_w_kx1"].reshape(split, taps)[:, ::-1],
        "k_h": inputs["L1_conv_w_1xk"].reshape(split, taps)[:, ::-1],
        "b_h": inputs["L1_conv_b_1xk"].reshape(1, split),
        "b_v": inputs["L1_conv_b_kx1"].reshape(1, split),
        "w1t": inputs["L1_conv_w1"].reshape(C, C).T,
        "b1": inputs["L1_conv_b1"].reshape(C, 1),
        "ident": _np.eye(C, dtype=_np.float32),
        "group_avg": (0.25 * (ch[:, None] // 2 == ch[None, :] // 2)).astype(_np.float32),
        "pick": _np.eye(2 * C, split, dtype=_np.float32),
        "x1_sel": _np.stack([sel, ~sel], 1).astype(_np.float32),
    }
    arrays = {k: _np.ascontiguousarray(a) for k, a in arrays.items()}
    nc = _bacc.Bacc("TRN2", target_bir_lowering=False, num_devices=1)
    args = [nc.dram_tensor(f"in_{k}", a.shape, mybir.dt.from_np(a.dtype), kind="ExternalInput").ap()
            for k, a in arrays.items()]
    args.append(nc.dram_tensor("out_y", x.shape, F32, kind="ExternalOutput").ap())
    conv_preact_kernel(nc, *args)
    r = _run(nc, [{f"in_{k}": a for k, a in arrays.items()}], core_ids=[0])
    return r.results[0]["out_y"]
```

```python
from contextlib import ExitStack

import concourse.bass as bass
from concourse import mybir

F32 = mybir.dt.float32
F16 = mybir.dt.float16
U8 = mybir.dt.uint8
ALU = mybir.AluOpType
ACT = mybir.ActivationFunctionType
AX = mybir.AxisListType

P = 128
PSUM_COLS = 512


def conv_preact_kernel(nc, x, w_co, w_ci, bias0, cmask, imask, k_v, k_h, b_h, b_v, w1t, b1,
                       ident, group_avg, pick, x1_sel, out):
    NI, C, H, W = x.shape
    NB = H // 2
    BL = 4
    CH = NB // BL
    UN = 4
    TI = CH // UN
    SPLIT = k_v.shape[0]
    K = k_v.shape[1]
    PAD = K // 2
    HH = H // 2
    BAND = HH + PAD
    TW = BAND + PAD
    ZW = W + 2
    ST = 4
    SA = 8
    N = 2 * W
    ZS = 64.0
    WS = 512.0
    assert SA % 4 == 0 and ST * UN <= CH - SA - 2 and SPLIT == 2 * SA
    assert CH * BL == NB and TI * UN == CH and HH == NB and 2 * C == P and H == W and UN == 4

    rows = "c (b two) w -> two c b w"
    s_dram = nc.dram_tensor("s_x1_split", (SPLIT, NB + 1, 2, W), F32, kind="Internal").ap()
    d_dram = nc.dram_tensor("s_dw_out", (SPLIT, H, W), F32, kind="Internal").ap()
    skew = nc.dram_tensor("s_taps", (2 * SPLIT, HH, 2 * P + 1), F32, kind="Internal")
    s_rows = s_dram.rearrange("c b two w -> c (b two) w")
    d_blocks = d_dram.rearrange(rows, two=2)

    with ExitStack() as ctx:
        def sb(name, shape, dt=F32):
            return ctx.enter_context(nc.sbuf_tensor(name, shape, dt))

        def sem(name):
            return ctx.enter_context(nc.semaphore(name))

        x1 = sb("x1", [P, NB + 1, W])
        xt = sb("xt", [P, 4, BL + 1, W])
        z32 = sb("z32", [P, 2, BL, W])
        zh = sb("zh", [P, 2, BL + 1, ZW], F16)
        zl = sb("zl", [P, 2, BL + 1, ZW], F16)
        xs = sb("xs", [P, 2, BL, W])
        gt = sb("gt", [P, 2, BL, W])
        toe = sb("toe", [HH, 2 * SPLIT, TW])
        zt = sb("zt", [HH, 4, 2, W])
        pa = sb("pa", [HH, 4, 2, W])
        dt_ = sb("dwt", [HH, 4, 2, W])
        wt = sb("wt", [P, 2, 2, 3, P], F16)
        w1bd = sb("w1bd", [P, P])
        w1n = sb("w1n", [P, P])
        gavg = sb("gavg", [P, P])
        ones = sb("ones", [P, P])
        pick_sb = sb("pick_sb", [P, SPLIT])
        sel = sb("sel", [P, 2])
        st1 = sb("st1", [P, 2 * CH, 6])
        st2 = sb("st2", [P, 2 * CH, 6])
        mv = sb("mv", [P, 2, 2])
        v = sb("v", [P, 40])
        bcin = sb("bcin", [P, 2 * SPLIT])
        bc = sb("bc", [P, 2 * SPLIT])
        dbias = sb("dbias", [HH, SPLIT, 2])
        m8 = sb("m8", [P, 2], U8)
        bhv = sb("bhv", [1, 2, SPLIT])
        zrow = sb("zrow", [P, ZW], F16)
        ps = ctx.enter_context(nc.psum_tensor("ps", [P, 8, PSUM_COLS], F32))

        def col(k):
            return v[:, k:k + 1]

        (B0, B1, SOUT, MINV, MAXV, AMAX, RAMAX, CM, IM, M1, R1, NB1, RS2, SH2, BU, T0, T1,
         PW) = range(18)
        (MU, DM, SQ, VE, R0, NT), (MU2, DM2, SQ2, VE2, R02, NT2) = range(18, 24), range(24, 30)
        GATE, GATE2 = 30, 31

        wco_sb = x1[:, 1:4, :].rearrange("p a b -> p (a b)")[:, 0:9 * C]
        wci_sb = x1[:, 4:7, :].rearrange("p a b -> p (a b)")[:, 0:9 * C].rearrange("p (t c) -> p t c", c=C)
        wsc = x1[:, 7:10, :].rearrange("p a b -> p (a b)")[:, 0:9 * C].rearrange("p (t c) -> p t c", c=C)
        rb = x1[:, 10, 0:C]
        idn = x1[0:C, 11, 0:C]
        dia = x1[0:C, 12, 0:C]
        wlo = x1[:, 13:16, :].rearrange("p a b -> p (a b)")[:, 0:9 * C].rearrange("p (t c) -> p t c", c=C)
        taps = x1[0:2 * SPLIT, 20:22, :].rearrange("p a b -> p (a b)")[:, 0:2 * P]
        vsum = x1[0:HH, 24:24 + SPLIT, :]
        whi = zh[:, 0, :, :].rearrange("p a b -> p (a b)")[:, 0:9 * C].rearrange("p (t c) -> p t c", c=C)

        params_in, taps_in, taps_out, toe_in = map(sem, ("params_in", "taps_in", "taps_out", "toe_in"))
        prep = sem("prep")
        prep_pe = sem("prep_pe")
        x_in = [sem(f"x_in{k}") for k in range(4)]
        s_in = [sem(f"s_in{k}") for k in range(2)]
        stat_used = sem("stat_used")
        zh_done, z32_done = sem("zh_done"), sem("z32_done")
        zl_done, conv_done, evac_done = sem("zl_done"), sem("conv_done"), sem("evac_done")
        halo_done = sem("halo_done")
        st2_done, saved = sem("st2_done"), sem("saved")
        g1_step, g1_mm, g1_pow = sem("g1_step"), sem("g1_mm"), sem("g1_pow")
        g2_step, g2_mm, g2_pow = sem("g2_step"), sem("g2_mm"), sem("g2_pow")
        zt_in = [sem(f"zt_in{k}") for k in range(4)]
        znorm, va_done = sem("znorm"), sem("va_done")
        pa_done, vb_done, dw_done = sem("pa_done"), sem("vb_done"), sem("dw_done")
        d_out = [sem(f"d_out{k}") for k in range(4)]
        d_in = [sem(f"d_in{k}") for k in range(4)]
        r_in = [sem(f"r_in{k}") for k in range(4)]
        mix_done = sem("mix_done")
        gelu_done, sum_done = sem("gelu_done"), sem("sum_done")
        o_out = [sem(f"o_out{k}") for k in range(2)]

        G1_STEPS, G1_MMS = 11, 2
        G2_STEPS, G2_MMS = 15, 4
        QS = SPLIT // 4

        block = ctx.enter_context(nc.Block())

        def static(t):
            return isinstance(t, int)

        def steps(eng, step, peel_first=False, looped=ST):
            if peel_first:
                for u in range(UN):
                    step(0, u)
            with eng.Fori(int(peel_first), looped) as t:
                for u in range(UN):
                    step(t, u)
            for t in range(looped, TI):
                for u in range(UN):
                    step(t, u)

        def images(eng, phase, between):
            phase(-1, False, True, True)
            with eng.Fori(0, NI - 2) as n:
                between(n, True, True)
                phase(n, True, True, True)
            between(NI - 2, True, False)
            phase(NI - 2, True, True, False)
            between(NI - 1, False, False)
            phase(NI - 1, True, False, False)

        @block.sync
        def _(sp):
            def load_stats(m, k, slot):
                xb = x[m].rearrange(rows, two=2)
                sp.wait_ge(stat_used, m * CH + k + 2)
                for par in range(2):
                    sp.dma_start(xs[64 * par:64 * par + 64, slot], xb[par][:, bass.ds(k * BL, BL), :]
                                 ).then_inc(s_in[slot], 16)

            def load_x(m, t, u):
                j = UN * t + u
                xb = x[m].rearrange(rows, two=2)
                sp.dma_start(xt[0:64, u, 1:BL + 1], xb[0][:, bass.ds(j * BL, BL), :]).then_inc(x_in[u], 16)
                if static(t) and j == 0:
                    sp.dma_start(xt[64:128, u, 1:BL + 1], xb[1][:, 0:BL, :]).then_inc(x_in[u], 16)
                else:
                    sp.dma_start(xt[64:128, u, :], xb[1][:, bass.ds(j * BL - 1, BL + 1), :]).then_inc(x_in[u], 16)

            def save(m, t, u):
                j = UN * t + u
                sp.wait_ge(evac_done, m * CH + j + 3)
                sp.dma_start(s_dram[:, bass.ds(j * BL + 1, BL), 0, :], x1[0:SPLIT, bass.ds(j * BL + 1, BL), :]
                             ).then_inc(saved, 16)
                k = BL + (static(t) and j == CH - 1)
                sp.dma_start(s_dram[:, bass.ds(j * BL, k), 1, :], x1[64:64 + SPLIT, bass.ds(j * BL, k), :]
                             ).then_inc(saved, 16)

            def to_x1(src_even, src_odd, j, s):
                sp.dma_start(x1[0:SPLIT, bass.ds(j * BL + 1, BL), :], src_even).then_inc(s, 16)
                sp.dma_start(x1[64:64 + SPLIT, bass.ds(j * BL + 1, BL), :], src_odd).then_inc(s, 16)

            def load_d(t, u):
                j = UN * t + u
                b = bass.ds(j * BL, BL)
                to_x1(d_blocks[0][:, b, :], d_blocks[1][:, b, :], j, d_in[u])

            def restore(t, u):
                j = UN * t + u
                b = bass.ds(j * BL + 1, BL)
                to_x1(s_dram[:, b, 0, :], s_dram[:, b, 1, :], j, r_in[u])

            for k in range(2):
                load_stats(0, k, k)
            for par in range(2):
                h = slice(64 * par, 64 * par + 64)
                masks = [m.bitcast(U8).rearrange("a c -> c a") for m in (cmask, imask)]
                for dst, src in ((wco_sb[h], w_co), (wci_sb[h], w_ci), (v[h, B0:B0 + 1], bias0),
                                 (v[h, B1:B1 + 1], b1), (m8[h, 0:1], masks[0]), (m8[h, 1:2], masks[1])):
                    sp.dma_start(dst, src).then_inc(params_in, 16)
            sp.dma_start(idn, ident).then_inc(params_in, 16)
            sp.dma_start(gavg[:], group_avg).then_inc(params_in, 16)
            sp.dma_start(pick_sb[:], pick).then_inc(params_in, 16)
            sp.dma_start(sel[:], x1_sel).then_inc(params_in, 16)
            sp.dma_start(bhv[:, 0, :], b_h).then_inc(params_in, 16)
            sp.dma_start(bhv[:, 1, :], b_v).then_inc(params_in, 16)
            with sp.Fori(1, CH // 2) as t:
                for u in range(2):
                    load_stats(0, 2 * t + u, u)
            for u in range(UN - 1):
                load_x(0, 0, u)
            with sp.Fori(0, SA // 2 + 1) as t:
                for u in range(2):
                    load_stats(1, 2 * t + u, u)
            sp.wait_ge(prep, 1)
            off = HH - 1
            sp.dma_start(taps[0:SPLIT, off:off + K], k_v).then_inc(taps_in, 16)
            sp.dma_start(taps[SPLIT:2 * SPLIT, off:off + K], k_h).then_inc(taps_in, 16)
            sp.dma_start(w1bd[0:64, 0:64], w1t).then_inc(taps_in, 16)
            sp.dma_start(w1bd[64:128, 64:128], w1t).then_inc(taps_in, 16)
            sp.wait_ge(taps_in, 64)
            sp.dma_start(skew.ap()[:, :, 0:2 * P],
                         taps.rearrange("f (a k) -> f a k", a=1).broadcast_to([2 * SPLIT, HH, 2 * P])
                         ).then_inc(taps_out, 16)
            sp.wait_ge(taps_out, 16)
            sp.dma_start(toe[:], bass.AP(skew, off, [[2 * P, HH], [HH * (2 * P + 1), 2 * SPLIT], [1, TW]])
                         ).then_inc(toe_in, 16)

            def phase(n, mix, conv, stats):
                m = n + 1

                def step(t, u):
                    j = UN * t + u
                    if conv:
                        if not (static(t) and t == 0 and u == 0):
                            save(m, t + (u + 3) // UN - 1, (u + 3) % UN)
                        if not (static(t) and j >= CH - 3):
                            load_x(m, t + (u + 3) // UN, (u + 3) % UN)
                        elif stats:
                            load_x(m + 1, 0, j - (CH - 3))
                    if mix:
                        sp.wait_ge(mix_done, n * CH + j + 1)
                        restore(t, u)
                        if not (static(t) and t == TI - 1):
                            load_d(t + 1, u)
                    if stats and not (static(t) and j >= CH - SA - 2):
                        load_stats(m + 1, j + SA + 2, u % 2)

                steps(sp, step, peel_first=True)

            def between(n, conv, stats):
                save(n, TI - 1, UN - 1)
                sp.wait_ge(saved, (n + 1) * 32 * CH)

                def load_plane(q, u):
                    sp.dma_start(zt[:, u], s_rows[bass.ds(4 * q + u, 1), 2:2 + H, :].rearrange(
                        "a (m p) w -> p (a m) w", m=2)).then_inc(zt_in[u], 16)

                def store_plane(q, u):
                    c = 4 * q + u
                    sp.wait_ge(dw_done, n * SPLIT + c + 3)
                    sp.dma_start(d_dram[bass.ds(c, 1)].rearrange("a (m p) w -> p (a m) w", m=2), dt_[:, u]
                                 ).then_inc(d_out[u], 16)

                def stats_after(q, u):
                    if stats and u % 2:
                        load_stats(n + 2, 2 * q + u // 2 + 2, u // 2)

                for u in range(4):
                    load_plane(0, u)
                if stats:
                    for k in range(2):
                        load_stats(n + 2, k, k)
                with sp.Fori(0, QS - 1) as q:
                    for u in range(4):
                        store_plane(q, u)
                        load_plane(q + 1, u)
                        stats_after(q, u)
                for u in range(4):
                    store_plane(QS - 1, u)
                    stats_after(QS - 1, u)
                for u in range(4):
                    sp.wait_ge(d_out[u], 1 + (n + 1) * 16 * QS)
                for u in range(UN):
                    load_d(0, u)

            images(sp, phase, between)
            for k in range(2):
                sp.wait_ge(o_out[k], 1 + 16 * CH * NI)

        @block.gpsimd
        def _(pool):
            def power(step, count, ve, r0, done):
                pool.wait_ge(step, count)
                nc.gpsimd.tensor_tensor(col(r0), col(ve), col(PW), ALU.pow).then_inc(done, 1)

            power(g1_step, 5, VE, R0, g1_pow)

            def phase(n, mix, conv, stats):
                if stats:
                    power(g1_step, G1_STEPS * (n + 2) + 5, VE, R0, g1_pow)

            def between(n, conv, stats):
                power(g2_step, G2_STEPS * n + 6, VE2, R02, g2_pow)

            images(pool, phase, between)

        def z_waits(eng, m, t, u):
            big = m * CH + UN * t + u
            eng.wait_ge(x_in[u], 32 * (TI * m + t + 1))
            eng.wait_ge(conv_done, big + 1)
            eng.wait_ge(halo_done, big + 1)

        @block.scalar
        def _(act):
            def z_high(m, t, u):
                j = UN * t + u
                z_waits(act, m, t, u)
                if static(t) and j == 0:
                    act.wait_ge(g1_step, G1_STEPS * (m + 1))
                nc.scalar.activation(zh[:, u % 2, 1:BL + 1, 1:W + 1], xt[:, u, 1:BL + 1, :], ACT.Identity,
                                     bias=col(NB1), scale=col(R1)).then_inc(zh_done, 1)
                a, b = (u + 1) % 2, u % 2
                if static(t) and j == 0:
                    nc.scalar.copy(zh[:, b, 0, :], zrow[:, :])
                    nc.scalar.copy(zl[:, b, 0, :], zrow[:, :]).then_inc(halo_done, 1)
                else:
                    act.wait_ge(zl_done, m * CH + j + 2)
                    act.wait_ge(zh_done, m * CH + j)
                    nc.scalar.copy(zh[:, b, 0, :], zh[:, a, BL, :])
                    nc.scalar.copy(zl[:, b, 0, :], zl[:, a, BL, :]).then_inc(halo_done, 1)

            z_high(0, 0, 0)
            z_high(0, 0, 1)

            def phase(n, mix, conv, stats):
                m = n + 1
                ob = out[n].rearrange(rows, two=2) if mix else None

                def step(t, u):
                    j = UN * t + u
                    if conv:
                        if not (static(t) and j >= CH - 2):
                            z_high(m, t + (u + 2) // UN, (u + 2) % UN)
                        elif stats and j == CH - 2:
                            z_high(m + 1, 0, 0)
                    if mix:
                        act.wait_ge(mix_done, n * CH + j + 1)
                        act.wait_ge(o_out[u % 2], 1 + 32 * ((CH // 2) * n + 2 * t + u // 2))
                        nc.scalar.activation(gt[:, u % 2].rearrange("p (g r) w -> p g (r w)", g=2), ps[:, 4:6, 0:N],
                                             ACT.Gelu, bias=col(BU), scale=1.0).then_inc(gelu_done, 1)
                        act.wait_ge(sum_done, n * CH + j + 2)
                        for par in range(2):
                            act.dma_start(ob[par][:, bass.ds(j * BL, BL), :], gt[64 * par:64 * par + 64, u % 2]
                                          ).then_inc(o_out[u % 2], 16)

                steps(act, step)

            def between(n, conv, stats):
                act.wait_ge(g2_step, G2_STEPS * (n + 1))

                def plane_norm(q, u):
                    c = 4 * q + u
                    act.wait_ge(zt_in[u], 16 * (QS * n + q + 1))
                    nc.scalar.activation(zt[:, u], zt[:, u], ACT.Identity, bias=bc[0:HH, bass.ds(c + SPLIT, 1)],
                                         scale=bc[0:HH, bass.ds(c, 1)]).then_inc(znorm, 1)

                def plane_turn(q, u):
                    c = 4 * q + u
                    act.wait_ge(va_done, n * SPLIT + c + 1)
                    act.wait_ge(vb_done, n * SPLIT + c + 1)
                    nc.scalar.copy(pa[:, u].rearrange("p m w -> p (m w)"), ps[0:HH, 2 + u, 0:N]
                                   ).then_inc(pa_done, 1)

                for u in range(3):
                    plane_norm(0, u)
                if conv:
                    z_high(n + 1, 0, 1)
                with act.Fori(0, QS - 1) as q:
                    for u in range(4):
                        plane_turn(q, u)
                        plane_norm(q + (u + 3) // 4, (u + 3) % 4)
                for u in range(4):
                    plane_turn(QS - 1, u)
                    if u == 0:
                        plane_norm(QS - 1, 3)

            images(act, phase, between)

        @block.tensor
        def _(pe):
            pe.wait_ge(prep, 8)
            nc.tensor.matmul(ps[:, 7, 0:C], ones[0:C, :], dia, start=True, stop=True).then_inc(prep_pe, 1)
            def group(step, count, mm, out_col, rhs):
                pe.wait_ge(step, count)
                nc.tensor.matmul(ps[:, 7, out_col:out_col + 1], gavg[:], rhs, start=True, stop=True).then_inc(mm, 1)

            def conv_chunk(m, t, u):
                j = UN * t + u
                big = m * CH + j
                pe.wait_ge(zh_done, big + 1)
                pe.wait_ge(zl_done, big + 3)
                pe.wait_ge(halo_done, big + 2)
                pe.wait_ge(evac_done, big + 1)
                z = u % 2
                terms = [(hl, zz, a, kx) for hl, zz in ((0, zh), (0, zl), (1, zh))
                         for a in range(2) for kx in range(3)]
                for k, (hl, zz, a, kx) in enumerate(terms):
                    for g in range(2):
                        ins = nc.tensor.matmul(ps[:, 2 * z + g, 0:N], wt[:, hl, a, kx, :],
                                               zz[:, z, 2 * g + a:2 * g + a + 2, kx:kx + W],
                                               start=(k == 0), stop=(k == len(terms) - 1))
                if static(t) and j == CH - 1:
                    terms = [q for q in terms if q[2] == 0]
                    for k, (hl, zz, a, kx) in enumerate(terms):
                        ins = nc.tensor.matmul(ps[:, 6, 0:W], wt[:, hl, 0, kx, :], zz[:, z, BL, kx:kx + W],
                                               start=(k == 0), stop=(k == len(terms) - 1))
                ins.then_inc(conv_done, 1)

            def mix_chunk(n, t, u):
                j = UN * t + u
                pe.wait_ge(d_in[u], 32 * (TI * n + t + 1))
                pe.wait_ge(gelu_done, n * CH + j + 1)
                for g in range(2):
                    ins = nc.tensor.matmul(ps[:, 4 + g, 0:N], w1n[:], x1[:, bass.ds(j * BL + 1 + 2 * g, 2), :],
                                           start=True, stop=True)
                ins.then_inc(mix_done, 1)


            group(g1_step, 1, g1_mm, 0, mv[:, 0, 0:1])
            group(g1_step, 4, g1_mm, 1, col(VE))
            conv_chunk(0, 0, 0)
            pe.wait_ge(toe_in, 16)
            for c in range(SPLIT):
                if c >= 2:
                    pe.wait_ge(prep, 14 + c - 1)
                o = ps[0:HH, 4 + c % 2, :]
                nc.tensor.matmul(o[:, 0:BAND], ones[0:HH, 0:HH], toe[:, c, PAD:TW], start=True, stop=False,
                                 skip_group_check=True)
                nc.tensor.matmul(o[:, H - BAND:H], ones[0:HH, 0:HH], toe[:, c, 0:BAND], start=False, stop=True,
                                 skip_group_check=True).then_inc(prep_pe, 1)
            for c in range(SPLIT):
                pe.wait_ge(prep, 14 + c + 1)
                for m in range(2):
                    o = ps[0:HH, 6, 2 * c + m:2 * c + m + 1]
                    nc.tensor.matmul(o, vsum[0:1, c, m * HH:(m + 1) * HH], bhv[:, 0, c:c + 1],
                                     start=True, stop=False)
                    ins = nc.tensor.matmul(o, ones[0:1, 0:HH], bhv[:, 1, c:c + 1], start=False, stop=True)
            ins.then_inc(prep_pe, 1)


            def phase(n, mix, conv, stats):
                m = n + 1
                if conv:
                    conv_chunk(m, 0, 1)
                if mix:
                    mix_chunk(n, 0, 0)

                def step(t, u):
                    j = UN * t + u
                    if mix and not (static(t) and j == CH - 1):
                        mix_chunk(n, t + (u + 1) // UN, (u + 1) % UN)
                    if conv and not (static(t) and j >= CH - 2):
                        conv_chunk(m, t + (u + 2) // UN, (u + 2) % UN)
                    if stats and static(t) and j == CH - SA:
                        group(g1_step, G1_STEPS * (m + 1) + 1, g1_mm, 0, mv[:, 0, 0:1])
                    if stats and static(t) and j == CH - SA + 2:
                        group(g1_step, G1_STEPS * (m + 1) + 4, g1_mm, 1, col(VE))
                    if stats and static(t) and j == CH - 1:
                        conv_chunk(m + 1, 0, 0)

                steps(pe, step)

            def between(n, conv, stats):
                group(g2_step, G2_STEPS * n + 2, g2_mm, 2, mv[:, 1, 0:1])
                group(g2_step, G2_STEPS * n + 5, g2_mm, 3, col(VE2))
                pe.wait_ge(g2_step, G2_STEPS * n + 13)
                nc.tensor.matmul(ps[:, 7, 4:5], w1bd[:], col(SH2), start=True, stop=True).then_inc(g2_mm, 1)
                nc.tensor.matmul(ps[:, 7, 8:8 + 2 * SPLIT], ones[:], bcin[:], start=True, stop=True
                                 ).then_inc(g2_mm, 1)

                def filtered(o, planes, band):
                    for m in range(2):
                        nc.tensor.matmul(o[:, m * H:m * H + BAND], planes[0][:, m * HH:(m + 1) * HH],
                                         band[:, 0, PAD:TW], start=(m == 0), stop=False, skip_group_check=True)
                        ins = nc.tensor.matmul(o[:, m * H + H - BAND:m * H + H], planes[1][:, m * HH:(m + 1) * HH],
                                               band[:, 0, 0:BAND], start=False, stop=(m == 1), skip_group_check=True)
                    return ins

                def vertical(q, u):
                    c = 4 * q + u
                    pe.wait_ge(znorm, n * SPLIT + c + 1)
                    pe.wait_ge(pa_done, n * SPLIT + c + 1)
                    filtered(ps[0:HH, 2 + u, :], [zt[:, u, k] for k in range(2)],
                             toe[:, bass.ds(c, 1), :]).then_inc(va_done, 1)

                def horizontal(q, u):
                    c = 4 * q + u
                    pe.wait_ge(pa_done, n * SPLIT + c + 5)
                    pe.wait_ge(dw_done, n * SPLIT + c + 1)
                    filtered(ps[0:HH, 6 + u % 2, :], [pa[:, u, k] for k in range(2)],
                             toe[:, bass.ds(c + SPLIT, 1), :]).then_inc(vb_done, 1)

                vertical(0, 0)
                vertical(0, 1)
                with pe.Fori(0, QS - 1) as q:
                    for u in range(4):
                        vertical(q + (u + 2) // 4, (u + 2) % 4)
                        horizontal(q, u)
                for u in range(4):
                    if u < 2:
                        vertical(QS - 1, u + 2)
                    horizontal(QS - 1, u)

            images(pe, phase, between)

        @block.vector
        def _(dve):
            dve_ = nc.vector

            def chunk_stats(m, k, slot, uses):
                dve.wait_ge(s_in[slot], 32 * ((CH // 2) * m + uses))
                for r in range(2):
                    ins = dve_.bn_stats(st1[:, bass.ds(2 * k + r, 1), :].rearrange("p a s -> p (a s)"),
                                        xs[:, slot, 2 * r:2 * r + 2, :])
                ins.then_inc(stat_used, 1)

            def step(ins):
                at[0] += 1
                ins.then_inc(prep, 1)
                dve.wait_ge(prep, at[0])

            at = [0]
            ahead = [(stat_used, 3), (zl_done, 2), (conv_done, 2), (evac_done, 2), (vb_done, 4), (pa_done, 4),
                     (dw_done, 2), (gelu_done, 1), (sum_done, 1)] + [(q, 1) for q in d_out + o_out]
            for k, (q, start) in enumerate(ahead):
                dve_.memset(dbias[:, k, :], 0.0).then_inc(q, start)
            dve_.memset(w1bd[:], 0.0)
            dve_.memset(ones[:], 1.0)
            dve_.memset(v[:, PW:PW + 1], -0.5)
            dve_.memset(x1[:, 0, :], 0.0)
            dve_.memset(xt[64:128, 0, 0, :], 0.0)
            dve_.memset(zl[:], 0.0)
            step(dve_.memset(taps, 0.0))
            with dve.Fori(0, CH // 2) as t:
                for u in range(2):
                    chunk_stats(0, 2 * t + u, u, t + 1)
            dve.wait_ge(params_in, 16 * 18)
            dve_.tensor_reduce(col(MAXV), wco_sb, AX.X, ALU.max)
            dve_.tensor_copy(v[:, CM:CM + 2], m8[:])
            step(dve_.tensor_reduce(col(MINV), wco_sb, AX.X, ALU.min))
            step(dve_.tensor_scalar(col(MINV), col(MINV), -1.0, 1e-30, ALU.mult, ALU.max))
            step(dve_.tensor_tensor(col(AMAX), col(MAXV), col(MINV), ALU.max))
            dve_.tensor_scalar(col(SOUT), col(AMAX), 1.0 / (WS * ZS), None, ALU.mult)
            step(dve_.reciprocal(col(RAMAX), col(AMAX)))
            step(dve_.tensor_scalar(col(RAMAX), col(RAMAX), col(CM), WS, ALU.mult, ALU.mult))
            dve_.tensor_scalar(col(B0), col(B0), col(CM), None, ALU.mult)
            step(dve_.tensor_scalar(dia, idn, v[0:C, RAMAX:RAMAX + 1], None, ALU.mult))
            step(dve_.tensor_scalar(wsc, wci_sb, col(IM), None, ALU.mult))
            dve.wait_ge(prep_pe, 1)
            step(dve_.tensor_copy(rb, ps[:, 7, 0:C]))
            step(dve_.tensor_tensor(wsc, wsc, rb.rearrange("p (a c) -> p a c", a=1).broadcast_to([P, 9, C]), ALU.mult))
            step(dve_.tensor_copy(whi, wsc))
            step(dve_.tensor_tensor(wlo, wsc, whi, ALU.subtract))
            assert at[0] == 12, at
            dve_.memset(zrow[:], 0.0)
            step(dve_.memset(wt[:], 0.0))
            taps_of = {(0, 0): (None, 0), (0, 1): (0, 1), (1, 0): (1, 2), (1, 1): (2, None)}
            for (a, par_in), kys in taps_of.items():
                h = slice(64 * par_in, 64 * par_in + 64)
                for m, ky in enumerate(kys):
                    if ky is not None:
                        dve_.tensor_copy(wt[h, 0, a, :, 64 * m:64 * m + 64], whi[h, 3 * ky:3 * ky + 3, :])
                        ins = dve_.tensor_copy(wt[h, 1, a, :, 64 * m:64 * m + 64], wlo[h, 3 * ky:3 * ky + 3, :])
            step(ins)
            dve_.memset(zh[:], 0.0).then_inc(halo_done, 1)


            def spread(link, mm, count, src, b, mu, dm, sq, ve):
                dve.wait_ge(mm, count)
                dve_.tensor_copy(col(mu), ps[:, 7, b:b + 1])
                link(dve_.tensor_tensor(col(dm), src[:, 0:1], ps[:, 7, b:b + 1], ALU.subtract))
                link(dve_.tensor_tensor(col(sq), col(dm), col(dm), ALU.mult))
                return dve_.tensor_tensor(col(ve), src[:, 1:2], col(sq), ALU.add)

            def newton(link, ve, r0, nt):
                link(dve_.tensor_tensor(col(nt), col(r0), col(r0), ALU.mult))
                link(dve_.tensor_tensor(col(nt), col(nt), col(ve), ALU.mult))
                link(dve_.tensor_scalar(col(nt), col(nt), -0.5, 1.5, ALU.mult, ALU.add))
                link(dve_.tensor_tensor(col(r0), col(r0), col(nt), ALU.mult))

            def gn1(m, stage):
                base = G1_STEPS * m
                done = [(0, 1, 3, 4, 5, 9)[stage]]

                def link(ins):
                    done[0] += 1
                    ins.then_inc(g1_step, 1)
                    dve.wait_ge(g1_step, base + done[0])

                if stage == 0:
                    dve.wait_ge(stat_used, 3 + (m + 1) * CH)
                    dve_.memset(col(GATE), 0.0)
                    dve_.bn_aggr(mv[:, 0, :], st1[:]).then_inc(g1_step, 1)
                elif stage == 1:
                    spread(link, g1_mm, G1_MMS * m + 1, mv[:, 0, :], 0, MU, DM, SQ, VE).then_inc(g1_step, 1)
                    dve.wait_ge(g1_step, base + 4)
                elif stage == 2:
                    done[0] = 4
                    dve.wait_ge(g1_mm, G1_MMS * m + 2)
                    link(dve_.tensor_scalar(col(VE), ps[:, 7, 1:2], 1e-5, None, ALU.add))
                elif stage == 3:
                    done[0] = 5
                    dve.wait_ge(g1_pow, m + 1)
                    newton(link, VE, R0, NT)
                else:
                    done[0] = 9
                    dve_.tensor_copy(col(M1), col(MU))
                    link(dve_.tensor_scalar(col(R1), col(R0), ZS, None, ALU.mult))
                    link(dve_.scalar_tensor_tensor(col(NB1), col(MU), -1.0, col(R1), ALU.mult, ALU.mult))
                    assert done[0] == G1_STEPS

            def z_low(m, t, u):
                big = m * CH + UN * t + u
                z_waits(dve, m, t, u)
                dve.wait_ge(zl_done, big + 1)
                dve_.tensor_scalar(z32[:, u % 2], xt[:, u, 1:BL + 1, :], col(M1), col(R1), ALU.subtract, ALU.mult
                                   ).then_inc(z32_done, 1)
                dve.wait_ge(z32_done, big + 1)
                dve.wait_ge(zh_done, big + 1)
                dve_.tensor_tensor(zl[:, u % 2, 1:BL + 1, 1:W + 1], z32[:, u % 2],
                                   zh[:, u % 2, 1:BL + 1, 1:W + 1], ALU.subtract).then_inc(zl_done, 1)

            for stage in range(5):
                gn1(0, stage)
            z_low(0, 0, 0)
            z_low(0, 0, 1)
            with dve.Fori(0, SA // 2) as t:
                for u in range(2):
                    chunk_stats(1, 2 * t + u, u, t + 1)
            for c in range(SPLIT):
                dve.wait_ge(prep_pe, 2 + c)
                step(dve_.tensor_copy(vsum[:, c, :], ps[0:HH, 4 + c % 2, 0:H]))
            dve.wait_ge(prep_pe, 2 + SPLIT)
            dve_.tensor_copy(dbias[:].rearrange("p c m -> p (c m)"), ps[0:HH, 6, 0:2 * SPLIT])
            def phase(n, mix, conv, stats):
                m = n + 1

                def add(t, u):
                    j = UN * t + u
                    dve.wait_ge(gelu_done, n * CH + j + 2)
                    dve.wait_ge(r_in[u], 32 * (TI * n + t + 1))
                    dve_.scalar_tensor_tensor(gt[:, u % 2], gt[:, u % 2], col(B0), x1[:, bass.ds(j * BL + 1, BL), :],
                                              ALU.add, ALU.add).then_inc(sum_done, 1)

                def conv_out(t, u):
                    j = UN * t + u
                    tail = static(t) and j == CH - 1
                    if mix:
                        dve.wait_ge(sum_done, n * CH + j + 2)
                    dve.wait_ge(conv_done, m * CH + j + 3)
                    s = slice(0, 64), slice(64, 128)
                    for g in range(2):
                        for par in range(2):
                            h = s[par]
                            a = 2 * g + 1 - par
                            ins = dve_.scalar_tensor_tensor(
                                x1[h, bass.ds(j * BL + a, 2), :],
                                ps[h, 2 * (u % 2) + g, 0:N].rearrange("p (r w) -> p r w", r=2),
                                v[h, SOUT:SOUT + 1], xt[h, u, a:a + 2, :], ALU.mult, ALU.add)
                    if tail:
                        ins = dve_.scalar_tensor_tensor(x1[s[1], NB, :], ps[s[1], 6, 0:W], v[s[1], SOUT:SOUT + 1],
                                                        xt[s[1], u, BL, :], ALU.mult, ALU.add)
                    ins.then_inc(evac_done, 1)
                    dve.wait_ge(evac_done, m * CH + j + 3)
                    for r in range(2):
                        ins = dve_.bn_stats(st2[:, bass.ds(2 * j + r, 1), :].rearrange("p a s -> p (a s)"),
                                            x1[:, bass.ds(j * BL + 2 * r, 2), :])
                    if tail:
                        ins.then_inc(st2_done, 1)
                        dve.wait_ge(st2_done, 2 * m + 1)
                        dve_.bn_stats(st2[:, 0, :], x1[:, 1:NB + 1:NB - 1, :]).then_inc(st2_done, 1)

                def step(t, u):
                    j = UN * t + u
                    if conv:
                        if not (static(t) and j >= CH - 2):
                            z_low(m, t + (u + 2) // UN, (u + 2) % UN)
                        elif stats and j == CH - 2:
                            z_low(m + 1, 0, 0)
                    if stats and not (static(t) and j >= CH - SA):
                        chunk_stats(m + 1, j + SA, u % 2, SA // 2 + 2 * t + u // 2 + 1)
                    if mix:
                        add(t, u)
                    if conv:
                        conv_out(t, u)
                    if stats and static(t):
                        at = {CH - SA: [0], CH - SA + 2: [1], CH - SA + 4: [2], CH - 3: [3, 4]}
                        for stage in at.get(j, []):
                            gn1(m + 1, stage)

                steps(dve, step)

            def between(n, conv, stats):
                base = G2_STEPS * n
                done = [0]

                def link(ins):
                    done[0] += 1
                    ins.then_inc(g2_step, 1)
                    dve.wait_ge(g2_step, base + done[0])

                dve.wait_ge(st2_done, 2 * n + 2)
                dve_.memset(col(GATE2), 0.0)
                link(dve_.bn_aggr(mv[:, 1, :], st2[:]))
                link(dve_.tensor_tensor(mv[:, 1, 0:1], mv[:, 1, 0:1], col(B0), ALU.add))
                link(spread(link, g2_mm, G2_MMS * n + 1, mv[:, 1, :], 2, MU2, DM2, SQ2, VE2))
                dve.wait_ge(g2_mm, G2_MMS * n + 2)
                link(dve_.tensor_scalar(col(VE2), ps[:, 7, 3:4], 1e-5, None, ALU.add))
                dve.wait_ge(g2_pow, n + 1)
                newton(link, VE2, R02, NT2)
                link(dve_.tensor_tensor(col(T0), col(B0), col(MU2), ALU.subtract))
                link(dve_.tensor_tensor(col(T1), col(T0), col(R02), ALU.mult))
                dve_.tensor_scalar(bcin[:, 0:SPLIT], pick_sb[:], col(R02), None, ALU.mult)
                dve_.tensor_scalar(bcin[:, SPLIT:2 * SPLIT], pick_sb[:], col(T1), None, ALU.mult)
                dve_.tensor_tensor(col(SH2), col(T1), sel[:, 1:2], ALU.mult)
                link(dve_.scalar_tensor_tensor(col(RS2), col(R02), sel[:, 1:2], sel[:, 0:1], ALU.mult, ALU.add))
                link(dve_.tensor_scalar(w1n[:], w1bd[:], col(RS2), None, ALU.mult))
                dve.wait_ge(g2_mm, G2_MMS * n + 4)
                dve_.tensor_tensor(col(BU), ps[:, 7, 4:5], col(B1), ALU.add)
                dve_.tensor_copy(bc[:], ps[:, 7, 8:8 + 2 * SPLIT]).then_inc(g2_step, 1)
                assert done[0] + 1 == G2_STEPS, done

                def plane_out(q, u):
                    c = 4 * q + u
                    dve.wait_ge(vb_done, n * SPLIT + c + 5)
                    dve.wait_ge(d_out[u], 1 + 16 * (QS * n + q))
                    bias = dbias[:, bass.ds(c, 1), :].rearrange("p a m -> p (a m)").rearrange("p (m a) -> p m a", a=1)
                    dve_.tensor_tensor(dt_[:, u], ps[0:HH, 6 + u % 2, 0:N].rearrange("p (m w) -> p m w", m=2),
                                       bias.broadcast_to([HH, 2, W]), ALU.add).then_inc(dw_done, 1)

                if conv:
                    z_low(n + 1, 0, 1)
                with dve.Fori(0, QS) as q:
                    for u in range(4):
                        plane_out(q, u)
                        if stats and u % 2:
                            chunk_stats(n + 2, 2 * q + u // 2, u // 2, q + 1)

            images(dve, phase, between)


def kernel(**inputs):
    import numpy as _np
    import concourse.bacc as _bacc
    from concourse.bass_utils import run_bass_kernel_spmd as _run

    x = _np.ascontiguousarray(inputs["x"])
    w = _np.asarray(inputs["L0_conv_weight"])
    C = w.shape[0]
    split, taps = inputs["L1_conv_w_1xk"].shape[0], inputs["L1_conv_w_1xk"].shape[3]
    ch = _np.arange(2 * C) % C
    sel = (ch < split)
    arrays = {
        "x": x,
        "w_co": w.reshape(C, -1),
        "w_ci": w.transpose(1, 2, 3, 0).reshape(C, -1, C),
        "bias0": inputs["L0_conv_bias"].reshape(C, 1),
        "cmask": _np.asarray(inputs["L0_conv_channel_mask"]).view(_np.int32).reshape(1, -1),
        "imask": _np.asarray(inputs["L0_conv_input_channel_mask"]).view(_np.int32).reshape(1, -1),
        "k_v": inputs["L1_conv_w_kx1"].reshape(split, taps)[:, ::-1],
        "k_h": inputs["L1_conv_w_1xk"].reshape(split, taps)[:, ::-1],
        "b_h": inputs["L1_conv_b_1xk"].reshape(1, split),
        "b_v": inputs["L1_conv_b_kx1"].reshape(1, split),
        "w1t": inputs["L1_conv_w1"].reshape(C, C).T,
        "b1": inputs["L1_conv_b1"].reshape(C, 1),
        "ident": _np.eye(C, dtype=_np.float32),
        "group_avg": (0.25 * (ch[:, None] // 2 == ch[None, :] // 2)).astype(_np.float32),
        "pick": _np.eye(2 * C, split, dtype=_np.float32),
        "x1_sel": _np.stack([sel, ~sel], 1).astype(_np.float32),
    }
    arrays = {k: _np.ascontiguousarray(a) for k, a in arrays.items()}
    nc = _bacc.Bacc("TRN2", target_bir_lowering=False, num_devices=1)
    args = [nc.dram_tensor(f"in_{k}", a.shape, mybir.dt.from_np(a.dtype), kind="ExternalInput").ap()
            for k, a in arrays.items()]
    args.append(nc.dram_tensor("out_y", x.shape, F32, kind="ExternalOutput").ap())
    conv_preact_kernel(nc, *args)
    r = _run(nc, [{f"in_{k}": a for k, a in arrays.items()}], core_ids=[0])
    return r.results[0]["out_y"]
```

```python
from contextlib import ExitStack

import concourse.bass as bass
from concourse import mybir

F32 = mybir.dt.float32
F16 = mybir.dt.float16
U8 = mybir.dt.uint8
ALU = mybir.AluOpType
ACT = mybir.ActivationFunctionType
AX = mybir.AxisListType

P = 128
PSUM_COLS = 512


def conv_preact_kernel(nc, x, w_co, w_ci, bias0, cmask, imask, k_v, k_h, b_h, b_v, w1t, b1,
                       ident, group_avg, pick, x1_sel, out):
    NI, C, H, W = x.shape
    NB = H // 2
    BL = 4
    CH = NB // BL
    UN = 4
    TI = CH // UN
    SPLIT = k_v.shape[0]
    K = k_v.shape[1]
    PAD = K // 2
    HH = H // 2
    BAND = HH + PAD
    TW = BAND + PAD
    ZW = W + 2
    ST = 4
    SA = 8
    N = 2 * W
    ZS = 64.0
    BIAS = 256
    WS = 512.0
    assert SA % 4 == 0 and ST * UN <= CH - SA - 2 and SPLIT == 2 * SA
    assert CH * BL == NB and TI * UN == CH and HH == NB and 2 * C == P and H == W and UN == 4

    rows = "c (b two) w -> two c b w"
    s_dram = nc.dram_tensor("s_x1_split", (SPLIT, NB + 1, 2, W), F32, kind="Internal").ap()
    d_dram = nc.dram_tensor("s_dw_out", (SPLIT, H, W), F32, kind="Internal").ap()
    skew = nc.dram_tensor("s_taps", (2 * SPLIT, HH, 2 * P + 1), F32, kind="Internal")
    s_rows = s_dram.rearrange("c b two w -> c (b two) w")
    d_blocks = d_dram.rearrange(rows, two=2)

    with ExitStack() as ctx:
        def sb(name, shape, dt=F32):
            return ctx.enter_context(nc.sbuf_tensor(name, shape, dt))

        def sem(name):
            return ctx.enter_context(nc.semaphore(name))

        x1 = sb("x1", [P, NB + 1, W])
        xt = sb("xt", [P, 4, BL + 1, W])
        z32 = sb("z32", [P, 2, BL, W])
        zh = sb("zh", [P, 2, BL + 1, ZW], F16)
        zl = sb("zl", [P, 2, BL + 1, ZW], F16)
        xs = sb("xs", [P, 2, BL, W])
        gt = sb("gt", [P, 2, BL, W])
        toe = sb("toe", [HH, 2 * SPLIT, TW])
        zt = sb("zt", [HH, 4, 2, W])
        pa = sb("pa", [HH, 4, 2, W])
        dt_ = sb("dwt", [HH, 4, 2, W])
        wt = sb("wt", [P, 2, 2, 3, P], F16)
        w1bd = sb("w1bd", [P, P])
        w1n = sb("w1n", [P, P])
        gavg = sb("gavg", [P, P])
        ones = sb("ones", [P, P])
        pick_sb = sb("pick_sb", [P, SPLIT])
        sel = sb("sel", [P, 2])
        st1 = sb("st1", [P, 2 * CH, 6])
        st2 = sb("st2", [P, 2 * CH, 6])
        mv = sb("mv", [P, 2, 2])
        v = sb("v", [P, 40])
        bcin = sb("bcin", [P, 2 * SPLIT])
        bc = sb("bc", [P, 2 * SPLIT])
        dbias = sb("dbias", [HH, SPLIT, 2])
        m8 = sb("m8", [P, 2], U8)
        bhv = sb("bhv", [1, 2, SPLIT])
        zrow = sb("zrow", [P, ZW], F16)
        ps = ctx.enter_context(nc.psum_tensor("ps", [P, 8, PSUM_COLS], F32))

        def col(k):
            return v[:, k:k + 1]

        (B0, B1, SOUT, MINV, MAXV, AMAX, RAMAX, CM, IM, M1, R1, NB1, RS2, SH2, BU, T0, T1,
         PW) = range(18)
        (MU, DM, SQ, VE, R0, NT), (MU2, DM2, SQ2, VE2, R02, NT2) = range(18, 24), range(24, 30)
        GATE, GATE2 = 30, 31

        wco_sb = x1[:, 1:4, :].rearrange("p a b -> p (a b)")[:, 0:9 * C]
        wci_sb = x1[:, 4:7, :].rearrange("p a b -> p (a b)")[:, 0:9 * C].rearrange("p (t c) -> p t c", c=C)
        wsc = x1[:, 7:10, :].rearrange("p a b -> p (a b)")[:, 0:9 * C].rearrange("p (t c) -> p t c", c=C)
        rb = x1[:, 10, 0:C]
        idn = x1[0:C, 11, 0:C]
        dia = x1[0:C, 12, 0:C]
        wlo = x1[:, 13:16, :].rearrange("p a b -> p (a b)")[:, 0:9 * C].rearrange("p (t c) -> p t c", c=C)
        taps = pa[0:2 * SPLIT, 0].rearrange("p a b -> p (a b)")[:, 0:2 * P]
        whi = zh[:, 0, :, :].rearrange("p a b -> p (a b)")[:, 0:9 * C].rearrange("p (t c) -> p t c", c=C)

        def vsum(c):
            home = (gt[:], dt_[:])[c // (SPLIT // 2)]
            return home.rearrange("p a b w -> p (a b) w")[:, c % (SPLIT // 2), :]

        SUMS = ST * UN
        PAIRS = SPLIT // 2
        assert SUMS + PAIRS + 2 < CH - 1

        first = [xs[:, 0], xs[:, 1], gt[:, 0], gt[:, 1]]
        assert CH // 4 == 7

        params_in, taps_in, taps_out, toe_in = map(sem, ("params_in", "taps_in", "taps_out", "toe_in"))
        prep = sem("prep")
        prep_pe = sem("prep_pe")
        x_in = [sem(f"x_in{k}") for k in range(4)]
        first_in = [sem(f"first_in{k}") for k in range(4)]
        s_in = [sem(f"s_in{k}") for k in range(2)]
        stat_used = sem("stat_used")
        zh_done, z32_done = sem("zh_done"), sem("z32_done")
        zl_done, conv_done, evac_done = sem("zl_done"), sem("conv_done"), sem("evac_done")
        halo_done = sem("halo_done")
        st2_done, saved = sem("st2_done"), sem("saved")
        g1_step, g1_mm, g1_pow = sem("g1_step"), sem("g1_mm"), sem("g1_pow")
        g2_step, g2_mm, g2_pow = sem("g2_step"), sem("g2_mm"), sem("g2_pow")
        zt_in = [sem(f"zt_in{k}") for k in range(4)]
        znorm, va_done = sem("znorm"), sem("va_done")
        pa_done, vb_done, dw_done = sem("pa_done"), sem("vb_done"), sem("dw_done")
        d_out = [sem(f"d_out{k}") for k in range(4)]
        d_in = [sem(f"d_in{k}") for k in range(4)]
        r_in = [sem(f"r_in{k}") for k in range(4)]
        mix_done = sem("mix_done")
        gelu_done, sum_done = sem("gelu_done"), sem("sum_done")
        o_out = [sem(f"o_out{k}") for k in range(4)]

        G1_STEPS, G1_MMS = 11, 2
        G2_STEPS, G2_MMS = 15, 4
        QS = SPLIT // 4

        block = ctx.enter_context(nc.Block())

        def static(t):
            return isinstance(t, int)

        def steps(eng, step, peel_first=False, looped=ST):
            if peel_first:
                for u in range(UN):
                    step(0, u)
            with eng.Fori(int(peel_first), looped) as t:
                for u in range(UN):
                    step(t, u)
            for t in range(looped, TI):
                for u in range(UN):
                    step(t, u)

        def images(eng, phase, between):
            phase(-1, False, True, True)
            with eng.Fori(0, NI - 2) as n:
                between(n, True, True)
                phase(n, True, True, True)
            between(NI - 2, True, False)
            phase(NI - 2, True, True, False)
            between(NI - 1, False, False)
            phase(NI - 1, True, False, False)

        def conv_bank(t, u):
            return 6 if static(t) and UN * t + u == 2 else 2 * (u % 2)

        def result(n, u):
            if last(n):
                return (gt if u < 2 else xs)[:, u % 2]
            return gt[:, u % 2]

        def last(n):
            return static(n) and n == NI - 1

        def loaded(n, u):
            return u | 1 if last(n) else u

        def mix_bank(n, u):
            return 4 + 2 * (u % 2) if last(n) else 4

        @block.sync
        def _(sp):
            def load_stats(m, k, slot):
                xb = x[m].rearrange(rows, two=2)
                sp.wait_ge(stat_used, m * CH + k + 2)
                for par in range(2):
                    sp.dma_start(xs[64 * par:64 * par + 64, slot], xb[par][:, bass.ds(k * BL, BL), :]
                                 ).then_inc(s_in[slot], 16)

            def load_x(m, t, u):
                j = UN * t + u
                xb = x[m].rearrange(rows, two=2)
                sp.dma_start(xt[0:64, u, 1:BL + 1], xb[0][:, bass.ds(j * BL, BL), :]).then_inc(x_in[u], 16)
                if static(t) and j == 0:
                    sp.dma_start(xt[64:128, u, 1:BL + 1], xb[1][:, 0:BL, :]).then_inc(x_in[u], 16)
                else:
                    sp.dma_start(xt[64:128, u, :], xb[1][:, bass.ds(j * BL - 1, BL + 1), :]).then_inc(x_in[u], 16)

            def save(m, t, u):
                j = UN * t + u
                sp.wait_ge(evac_done, m * CH + j + 3)
                sp.dma_start(s_dram[:, bass.ds(j * BL + 1, BL), 0, :], x1[0:SPLIT, bass.ds(j * BL + 1, BL), :]
                             ).then_inc(saved, 16)
                k = BL + (static(t) and j == CH - 1)
                sp.dma_start(s_dram[:, bass.ds(j * BL, k), 1, :], x1[64:64 + SPLIT, bass.ds(j * BL, k), :]
                             ).then_inc(saved, 16)

            def to_x1(n, t, u, even, odd, lead, s):
                if u != loaded(n, u):
                    return
                chunks = 2 if last(n) else 1
                b = (UN * t + u + 1 - chunks) * BL
                src = bass.ds(b + lead, chunks * BL)
                dst = bass.ds(b + 1, chunks * BL)
                sp.dma_start(x1[0:SPLIT, dst, :], even[:, src, :]).then_inc(s[u], 16)
                sp.dma_start(x1[64:64 + SPLIT, dst, :], odd[:, src, :]).then_inc(s[u], 16)

            def load_d(n, t, u):
                to_x1(n, t, u, d_blocks[0], d_blocks[1], 0, d_in)

            def restore(n, t, u):
                to_x1(n, t, u, s_dram[:, :, 0, :], s_dram[:, :, 1, :], 1, r_in)

            def load_first(t, u):
                k = 4 * t + u
                xb = x[0].rearrange(rows, two=2)
                if not (static(t) and t == 0):
                    sp.wait_ge(stat_used, k)
                for par in range(2):
                    sp.dma_start(first[u][64 * par:64 * par + 64], xb[par][:, bass.ds(k * BL, BL), :]
                                 ).then_inc(first_in[u], 16)

            for u in range(4):
                load_first(0, u)
            for par in range(2):
                h = slice(64 * par, 64 * par + 64)
                masks = [m.bitcast(U8).rearrange("a c -> c a") for m in (cmask, imask)]
                for dst, src in ((wco_sb[h], w_co), (wci_sb[h], w_ci), (v[h, B0:B0 + 1], bias0),
                                 (v[h, B1:B1 + 1], b1), (m8[h, 0:1], masks[0]), (m8[h, 1:2], masks[1])):
                    sp.dma_start(dst, src).then_inc(params_in, 16)
            sp.dma_start(idn, ident).then_inc(params_in, 16)
            sp.dma_start(gavg[:], group_avg).then_inc(params_in, 16)
            sp.dma_start(pick_sb[:], pick).then_inc(params_in, 16)
            sp.dma_start(sel[:], x1_sel).then_inc(params_in, 16)
            sp.dma_start(bhv[:, 0, :], b_h).then_inc(params_in, 16)
            sp.dma_start(bhv[:, 1, :], b_v).then_inc(params_in, 16)
            sp.wait_ge(prep, 1)
            off = HH - 1
            sp.dma_start(taps[0:SPLIT, off:off + K], k_v).then_inc(taps_in, 16)
            sp.dma_start(taps[SPLIT:2 * SPLIT, off:off + K], k_h).then_inc(taps_in, 16)
            sp.dma_start(w1bd[0:64, 0:64], w1t).then_inc(taps_in, 16)
            sp.dma_start(w1bd[64:128, 64:128], w1t).then_inc(taps_in, 16)
            with sp.Fori(1, CH // 4) as t:
                for u in range(4):
                    load_first(t, u)
            for u in range(UN - 1):
                load_x(0, 0, u)
            with sp.Fori(0, SA // 2 + 1) as t:
                for u in range(2):
                    load_stats(1, 2 * t + u, u)
            def skew_out():
                sp.wait_ge(taps_in, 64)
                sp.dma_start(skew.ap()[:, :, 0:2 * P],
                             taps.rearrange("f (a k) -> f a k", a=1).broadcast_to([2 * SPLIT, HH, 2 * P])
                             ).then_inc(taps_out, 16)

            def toe_back():
                sp.wait_ge(taps_out, 16)
                sp.dma_start(toe[:], bass.AP(skew, off, [[2 * P, HH], [HH * (2 * P + 1), 2 * SPLIT], [1, TW]])
                             ).then_inc(toe_in, 16)

            def phase(n, mix, conv, stats):
                m = n + 1

                def step(t, u):
                    j = UN * t + u
                    if mix and u == loaded(n, u):
                        sp.wait_ge(mix_done, n * CH + j + 1)
                        restore(n, t, u)
                        if not (static(t) and t == TI - 1):
                            load_d(n, t + 1, u)
                    if conv:
                        if not (static(t) and t == 0 and u == 0):
                            save(m, t + (u + 3) // UN - 1, (u + 3) % UN)
                        if not (static(t) and j >= CH - 3):
                            load_x(m, t + (u + 3) // UN, (u + 3) % UN)
                        elif stats:
                            load_x(m + 1, 0, j - (CH - 3))
                    if stats and not (static(t) and j >= CH - SA - 2):
                        load_stats(m + 1, j + SA + 2, u % 2)
                    if not mix and static(t) and j == 1:
                        skew_out()
                    if not mix and static(t) and j == 3:
                        toe_back()

                steps(sp, step, peel_first=True)

            def between(n, conv, stats):
                save(n, TI - 1, UN - 1)
                sp.wait_ge(saved, (n + 1) * 32 * CH)

                def load_plane(q, u):
                    sp.dma_start(zt[:, u], s_rows[bass.ds(4 * q + u, 1), 2:2 + H, :].rearrange(
                        "a (m p) w -> p (a m) w", m=2)).then_inc(zt_in[u], 16)

                def stats_ahead(k, slot):
                    if stats:
                        load_stats(n + 2, k, slot)

                def planes_ahead(q, first):
                    for u in range(4):
                        sp.wait_ge(va_done, n * SPLIT + 4 * q + u + 1)
                        load_plane(q + 1, u)
                        if u == 1 and not first:
                            stats_ahead(2 * q + 1, 1)
                        if u == 3:
                            stats_ahead(2 * q + 2, 0)

                for u in range(4):
                    load_plane(0, u)
                for k in range(2):
                    stats_ahead(k, k)
                planes_ahead(0, True)
                with sp.Fori(1, QS - 1) as q:
                    planes_ahead(q, False)
                stats_ahead(SA - 1, 1)
                stats_ahead(SA, 0)
                for u in range(4):
                    sp.wait_ge(d_out[u], 1 + (n + 1) * 16 * QS)
                for u in range(UN):
                    load_d(n, 0, u)
                stats_ahead(SA + 1, 1)

            images(sp, phase, between)
            for u in range(4):
                sp.wait_ge(o_out[u], 1 + 32 * TI * NI)

        @block.gpsimd
        def _(pool):
            def power(step, count, ve, r0, done):
                pool.wait_ge(step, count)
                nc.gpsimd.tensor_tensor(col(r0), col(ve), col(PW), ALU.pow).then_inc(done, 1)

            power(g1_step, 5, VE, R0, g1_pow)

            def phase(n, mix, conv, stats):
                if stats:
                    power(g1_step, G1_STEPS * (n + 2) + 5, VE, R0, g1_pow)

            def between(n, conv, stats):
                power(g2_step, G2_STEPS * n + 7, VE2, R02, g2_pow)

            images(pool, phase, between)

        def z_waits(eng, m, t, u):
            big = m * CH + UN * t + u
            eng.wait_ge(x_in[u], 32 * (TI * m + t + 1))
            eng.wait_ge(conv_done, big + 1)
            eng.wait_ge(halo_done, big + 1)

        @block.scalar
        def _(act):
            def z_high(m, t, u):
                j = UN * t + u
                z_waits(act, m, t, u)
                if static(t) and j == 0:
                    act.wait_ge(g1_step, G1_STEPS * (m + 1))
                nc.scalar.activation(zh[:, u % 2, 1:BL + 1, 1:W + 1], xt[:, u, 1:BL + 1, :], ACT.Identity,
                                     bias=col(NB1), scale=col(R1)).then_inc(zh_done, 1)
                a, b = (u + 1) % 2, u % 2
                if static(t) and j == 0:
                    nc.scalar.copy(zh[:, b, 0, :], zrow[:, :])
                    nc.scalar.copy(zl[:, b, 0, :], zrow[:, :]).then_inc(halo_done, 1)
                else:
                    act.wait_ge(zl_done, m * CH + j + 2)
                    act.wait_ge(zh_done, m * CH + j)
                    nc.scalar.copy(zh[:, b, 0, :], zh[:, a, BL, :])
                    nc.scalar.copy(zl[:, b, 0, :], zl[:, a, BL, :]).then_inc(halo_done, 1)

            z_high(0, 0, 0)
            z_high(0, 0, 1)

            def phase(n, mix, conv, stats):
                m = n + 1
                ob = out[n].rearrange(rows, two=2) if mix else None

                def step(t, u):
                    j = UN * t + u
                    if conv:
                        if not (static(t) and j >= CH - 2):
                            z_high(m, t + (u + 2) // UN, (u + 2) % UN)
                        elif stats and j == CH - 2:
                            z_high(m + 1, 0, 0)
                    if mix:
                        act.wait_ge(mix_done, n * CH + j + 1)
                        if last(n) and not (static(t) and t == 0 and u < 2):
                            act.wait_ge(o_out[u], 1 + 32 * (TI * n + t))
                        else:
                            act.wait_ge(o_out[(u + 2) % 4], 1 + 32 * (TI * n + t + u // 2))
                        nc.scalar.activation(result(n, u).rearrange("p (g r) w -> p g (r w)", g=2), ps[:, mix_bank(n, u):mix_bank(n, u) + 2, 0:N],
                                             ACT.Gelu, bias=col(BU), scale=1.0).then_inc(gelu_done, 1)
                        if not (static(t) and j < lag):
                            store(t + (u + UN - lag) // UN - 1, (u + UN - lag) % UN)

                lag = 2 if last(n) else 1

                def store(t, u):
                    j = UN * t + u
                    act.wait_ge(sum_done, n * CH + j + 2)
                    for par in range(2):
                        act.dma_start(ob[par][:, bass.ds(j * BL, BL), :], result(n, u)[64 * par:64 * par + 64]
                                      ).then_inc(o_out[u], 16)

                steps(act, step, peel_first=True)
                if mix:
                    for u in range(UN - lag, UN):
                        store(TI - 1, u)

            def between(n, conv, stats):
                act.wait_ge(g2_step, G2_STEPS * (n + 1))

                def plane_norm(q, u):
                    c = 4 * q + u
                    act.wait_ge(zt_in[u], 16 * (QS * n + q + 1))
                    nc.scalar.activation(zt[:, u], zt[:, u], ACT.Identity, bias=bc[0:HH, bass.ds(c + SPLIT, 1)],
                                         scale=bc[0:HH, bass.ds(c, 1)]).then_inc(znorm, 1)

                def plane_turn(q, u):
                    c = 4 * q + u
                    act.wait_ge(va_done, n * SPLIT + c + 1)
                    act.wait_ge(vb_done, n * SPLIT + c + 1)
                    nc.scalar.copy(pa[:, u].rearrange("p m w -> p (m w)"), ps[0:HH, 2 + u, 0:N]
                                   ).then_inc(pa_done, 1)

                for u in range(3):
                    plane_norm(0, u)
                if conv:
                    z_high(n + 1, 0, 1)

                def store_plane(q, u):
                    c = 4 * q + u
                    act.wait_ge(dw_done, n * SPLIT + c + 3)
                    act.dma_start(d_dram[bass.ds(c, 1)].rearrange("a (m p) w -> p (a m) w", m=2), dt_[:, u]
                                  ).then_inc(d_out[u], 16)

                def turns(q, first, last):
                    for u in range(4):
                        plane_turn(q, u)
                        if not (last and u):
                            plane_norm(q + (u + 3) // 4, (u + 3) % 4)
                        if u == 3 or not first:
                            store_plane(q + (u + 1) // 4 - 1, (u + 1) % 4)

                turns(0, True, False)
                with act.Fori(1, QS - 1) as q:
                    turns(q, False, False)
                turns(QS - 1, False, True)
                for u in range(1, 4):
                    store_plane(QS - 1, u)

            images(act, phase, between)

        @block.tensor
        def _(pe):
            pe.wait_ge(prep, 8)
            nc.tensor.matmul(ps[:, 7, 0:C], ones[0:C, :], dia, start=True, stop=True).then_inc(prep_pe, 1)
            def group(step, count, mm, out_col, rhs):
                pe.wait_ge(step, count)
                nc.tensor.matmul(ps[:, 7, out_col:out_col + 1], gavg[:], rhs, start=True, stop=True).then_inc(mm, 1)

            def conv_chunk(m, t, u, midway=None):
                j = UN * t + u
                big = m * CH + j
                pe.wait_ge(zh_done, big + 1)
                pe.wait_ge(zl_done, big + 3)
                pe.wait_ge(halo_done, big + 2)
                if not (static(t) and j == 2):
                    pe.wait_ge(evac_done, big + 1)
                elif not (static(m) and m == 0):
                    pe.wait_ge(dw_done, m * SPLIT + 2)
                z = u % 2
                bank = conv_bank(t, u)
                terms = [(hl, zz, a, kx) for hl, zz in ((0, zh), (0, zl), (1, zh))
                         for a in range(2) for kx in range(3)]
                for k, (hl, zz, a, kx) in enumerate(terms):
                    if midway and k == midway[0]:
                        midway[1]()
                    for g in range(2):
                        ins = nc.tensor.matmul(ps[:, bank + g, 0:N], wt[:, hl, a, kx, :],
                                               zz[:, z, 2 * g + a:2 * g + a + 2, kx:kx + W],
                                               start=(k == 0), stop=(k == len(terms) - 1))
                if static(t) and j == CH - 1:
                    terms = [q for q in terms if q[2] == 0]
                    for k, (hl, zz, a, kx) in enumerate(terms):
                        ins = nc.tensor.matmul(ps[:, 6, 0:W], wt[:, hl, 0, kx, :], zz[:, z, BL, kx:kx + W],
                                               start=(k == 0), stop=(k == len(terms) - 1))
                ins.then_inc(conv_done, 1)

            def mix_chunk(n, t, u):
                j = UN * t + u
                pe.wait_ge(d_in[loaded(n, u)], 32 * (TI * n + t + 1))
                pe.wait_ge(gelu_done, n * CH + j + (0 if last(n) and not (static(t) and j < 2) else 1))
                for g in range(2):
                    ins = nc.tensor.matmul(ps[:, mix_bank(n, u) + g, 0:N], w1n[:], x1[:, bass.ds(j * BL + 1 + 2 * g, 2), :],
                                           start=True, stop=True)
                ins.then_inc(mix_done, 1)


            group(g1_step, 1, g1_mm, 0, mv[:, 0, 0:1])
            group(g1_step, 4, g1_mm, 1, col(VE))
            conv_chunk(0, 0, 0)
            def column_sums(k):
                if k == 0:
                    pe.wait_ge(toe_in, 16)
                if k >= 2:
                    pe.wait_ge(prep, 14 + k - 1)
                for e in range(2):
                    o = ps[0:HH, 4 + k % 2, e * H:(e + 1) * H]
                    nc.tensor.matmul(o[:, 0:BAND], ones[0:HH, 0:HH], toe[:, 2 * k + e, PAD:TW], start=(e == 0),
                                     stop=False, skip_group_check=True)
                    ins = nc.tensor.matmul(o[:, H - BAND:H], ones[0:HH, 0:HH], toe[:, 2 * k + e, 0:BAND],
                                           start=False, stop=(e == 1), skip_group_check=True)
                ins.then_inc(prep_pe, 1)

            def filter_bias(k):
                pe.wait_ge(prep, 14 + k + 1)
                for c in (2 * k, 2 * k + 1):
                    for m in range(2):
                        ins = nc.tensor.matmul(ps[0:HH, 6, BIAS + 2 * c + m:BIAS + 2 * c + m + 1],
                                               vsum(c)[0:1, m * HH:(m + 1) * HH], ones[0:1, 0:1],
                                               start=True, stop=True)
                if k == PAIRS - 1:
                    ins.then_inc(prep_pe, 1)

            def phase(n, mix, conv, stats):
                m = n + 1
                if conv:
                    conv_chunk(m, 0, 1)
                if mix:
                    mix_chunk(n, 0, 0)

                def step(t, u):
                    j = UN * t + u

                    def product(ahead):
                        mix_chunk(n, t + (u + ahead) // UN, (u + ahead) % UN)

                    amid = None
                    if mix and conv and static(t):
                        amid = {0: (6, lambda: product(1)), CH - 3: (9, lambda: product(2))}.get(j)
                    if mix and not (static(t) and (j == CH - 1 or conv and j in (0, CH - 2))):
                        product(1)
                    if conv and not (static(t) and j >= CH - 2):
                        conv_chunk(m, t + (u + 2) // UN, (u + 2) % UN, midway=amid)
                    if stats and static(t) and j == CH - SA:
                        group(g1_step, G1_STEPS * (m + 1) + 1, g1_mm, 0, mv[:, 0, 0:1])
                    if stats and static(t) and j == CH - SA + 2:
                        group(g1_step, G1_STEPS * (m + 1) + 4, g1_mm, 1, col(VE))
                    if stats and static(t) and j == CH - 1:
                        conv_chunk(m + 1, 0, 0)
                    if not mix and static(t):
                        if SUMS <= j < SUMS + PAIRS:
                            column_sums(j - SUMS)
                        if SUMS + 2 <= j < SUMS + 2 + PAIRS:
                            filter_bias(j - SUMS - 2)

                steps(pe, step, peel_first=True)

            def between(n, conv, stats):
                group(g2_step, G2_STEPS * n + 2, g2_mm, 2, mv[:, 1, 0:1])
                group(g2_step, G2_STEPS * n + 5, g2_mm, 3, col(VE2))
                pe.wait_ge(g2_step, G2_STEPS * n + 13)
                nc.tensor.matmul(ps[:, 7, 4:5], w1bd[:], col(SH2), start=True, stop=True).then_inc(g2_mm, 1)
                nc.tensor.matmul(ps[:, 7, 8:8 + 2 * SPLIT], ones[:], bcin[:], start=True, stop=True
                                 ).then_inc(g2_mm, 1)

                def filtered(o, planes, band):
                    for m in range(2):
                        nc.tensor.matmul(o[:, m * H:m * H + BAND], planes[0][:, m * HH:(m + 1) * HH],
                                         band[:, 0, PAD:TW], start=(m == 0), stop=False, skip_group_check=True)
                        ins = nc.tensor.matmul(o[:, m * H + H - BAND:m * H + H], planes[1][:, m * HH:(m + 1) * HH],
                                               band[:, 0, 0:BAND], start=False, stop=(m == 1), skip_group_check=True)
                    return ins

                def vertical(q, u):
                    c = 4 * q + u
                    pe.wait_ge(znorm, n * SPLIT + c + 1)
                    pe.wait_ge(pa_done, n * SPLIT + c + 1)
                    filtered(ps[0:HH, 2 + u, :], [zt[:, u, k] for k in range(2)],
                             toe[:, bass.ds(c, 1), :]).then_inc(va_done, 1)

                def horizontal(q, u):
                    c = 4 * q + u
                    pe.wait_ge(pa_done, n * SPLIT + c + 5)
                    pe.wait_ge(dw_done, n * SPLIT + c + 1)
                    filtered(ps[0:HH, 6 + u % 2, :], [pa[:, u, k] for k in range(2)],
                             toe[:, bass.ds(c + SPLIT, 1), :]).then_inc(vb_done, 1)

                vertical(0, 0)
                vertical(0, 1)
                with pe.Fori(0, QS - 1) as q:
                    for u in range(4):
                        vertical(q + (u + 2) // 4, (u + 2) % 4)
                        horizontal(q, u)
                for u in range(4):
                    if u < 2:
                        vertical(QS - 1, u + 2)
                    horizontal(QS - 1, u)

            images(pe, phase, between)

        @block.vector
        def _(dve):
            dve_ = nc.vector

            def chunk_stats(m, k, slot, uses):
                dve.wait_ge(s_in[slot], 32 * ((CH // 2) * (m - 1) + uses))
                half_stats(k, xs[:, slot])

            def half_stats(k, chunk):
                for r in range(2):
                    ins = dve_.bn_stats(st1[:, bass.ds(2 * k + r, 1), :].rearrange("p a s -> p (a s)"),
                                        chunk[:, 2 * r:2 * r + 2, :])
                ins.then_inc(stat_used, 1)

            def first_stats(t):
                for u in range(4):
                    dve.wait_ge(first_in[u], 32 * (t + 1))
                    half_stats(4 * t + u, first[u])

            def step(ins):
                at[0] += 1
                ins.then_inc(prep, 1)
                dve.wait_ge(prep, at[0])

            at = [0]
            ahead = [(stat_used, 3), (zl_done, 2), (conv_done, 2), (evac_done, 2), (vb_done, 4), (pa_done, 4),
                     (dw_done, 2), (gelu_done, 1), (sum_done, 1)] + [(q, 1) for q in d_out + o_out]
            for k, (q, start) in enumerate(ahead):
                dve_.memset(bcin[:, k:k + 1], 0.0).then_inc(q, start)
            dve_.memset(w1bd[:], 0.0)
            dve_.memset(ones[:], 1.0)
            dve_.memset(v[:, PW:PW + 1], -0.5)
            dve_.memset(x1[:, 0, :], 0.0)
            dve_.memset(xt[64:128, 0, 0, :], 0.0)
            dve_.memset(zl[:], 0.0)
            step(dve_.memset(taps, 0.0))
            with dve.Fori(0, 2) as t:
                first_stats(t)
            dve.wait_ge(params_in, 16 * 18)
            dve_.tensor_reduce(col(MAXV), wco_sb, AX.X, ALU.max)
            dve_.tensor_copy(v[:, CM:CM + 2], m8[:])
            step(dve_.tensor_reduce(col(MINV), wco_sb, AX.X, ALU.min))
            step(dve_.tensor_scalar(col(MINV), col(MINV), -1.0, 1e-30, ALU.mult, ALU.max))
            step(dve_.tensor_tensor(col(AMAX), col(MAXV), col(MINV), ALU.max))
            dve_.tensor_scalar(col(SOUT), col(AMAX), 1.0 / (WS * ZS), None, ALU.mult)
            step(dve_.reciprocal(col(RAMAX), col(AMAX)))
            step(dve_.tensor_scalar(col(RAMAX), col(RAMAX), col(CM), WS, ALU.mult, ALU.mult))
            dve_.tensor_scalar(col(B0), col(B0), col(CM), None, ALU.mult)
            step(dve_.tensor_scalar(dia, idn, v[0:C, RAMAX:RAMAX + 1], None, ALU.mult))
            first_stats(2)
            step(dve_.tensor_scalar(wsc, wci_sb, col(IM), None, ALU.mult))
            dve.wait_ge(prep_pe, 1)
            step(dve_.tensor_copy(rb, ps[:, 7, 0:C]))
            step(dve_.tensor_tensor(wsc, wsc, rb.rearrange("p (a c) -> p a c", a=1).broadcast_to([P, 9, C]), ALU.mult))
            first_stats(3)
            step(dve_.tensor_copy(whi, wsc))
            step(dve_.tensor_tensor(wlo, wsc, whi, ALU.subtract))
            assert at[0] == 12, at
            first_stats(4)
            dve_.memset(zrow[:], 0.0)
            step(dve_.memset(wt[:], 0.0))
            first_stats(5)
            taps_of = {(0, 0): (None, 0), (0, 1): (0, 1), (1, 0): (1, 2), (1, 1): (2, None)}
            for (a, par_in), kys in taps_of.items():
                h = slice(64 * par_in, 64 * par_in + 64)
                for m, ky in enumerate(kys):
                    if ky is not None:
                        dve_.tensor_copy(wt[h, 0, a, :, 64 * m:64 * m + 64], whi[h, 3 * ky:3 * ky + 3, :])
                        ins = dve_.tensor_copy(wt[h, 1, a, :, 64 * m:64 * m + 64], wlo[h, 3 * ky:3 * ky + 3, :])
            step(ins)
            dve_.memset(zh[:], 0.0).then_inc(halo_done, 1)
            first_stats(6)


            def spread(link, mm, count, src, b, mu, dm, sq, ve):
                dve.wait_ge(mm, count)
                dve_.tensor_copy(col(mu), ps[:, 7, b:b + 1])
                link(dve_.tensor_tensor(col(dm), src[:, 0:1], ps[:, 7, b:b + 1], ALU.subtract))
                link(dve_.tensor_tensor(col(sq), col(dm), col(dm), ALU.mult))
                return dve_.tensor_tensor(col(ve), src[:, 1:2], col(sq), ALU.add)

            def newton(link, ve, r0, nt):
                link(dve_.tensor_tensor(col(nt), col(r0), col(r0), ALU.mult))
                link(dve_.tensor_tensor(col(nt), col(nt), col(ve), ALU.mult))
                link(dve_.tensor_scalar(col(nt), col(nt), -0.5, 1.5, ALU.mult, ALU.add))
                link(dve_.tensor_tensor(col(r0), col(r0), col(nt), ALU.mult))

            def gn1(m, stage):
                base = G1_STEPS * m
                done = [(0, 1, 3, 4, 5, 9)[stage]]

                def link(ins):
                    done[0] += 1
                    ins.then_inc(g1_step, 1)
                    dve.wait_ge(g1_step, base + done[0])

                if stage == 0:
                    dve.wait_ge(stat_used, 3 + (m + 1) * CH)
                    dve_.memset(col(GATE), 0.0)
                    dve_.bn_aggr(mv[:, 0, :], st1[:]).then_inc(g1_step, 1)
                elif stage == 1:
                    spread(link, g1_mm, G1_MMS * m + 1, mv[:, 0, :], 0, MU, DM, SQ, VE).then_inc(g1_step, 1)
                    dve.wait_ge(g1_step, base + 4)
                elif stage == 2:
                    done[0] = 4
                    dve.wait_ge(g1_mm, G1_MMS * m + 2)
                    link(dve_.tensor_scalar(col(VE), ps[:, 7, 1:2], 1e-5, None, ALU.add))
                elif stage == 3:
                    done[0] = 5
                    dve.wait_ge(g1_pow, m + 1)
                    newton(link, VE, R0, NT)
                else:
                    done[0] = 9
                    dve_.tensor_copy(col(M1), col(MU))
                    link(dve_.tensor_scalar(col(R1), col(R0), ZS, None, ALU.mult))
                    link(dve_.scalar_tensor_tensor(col(NB1), col(MU), -1.0, col(R1), ALU.mult, ALU.mult))
                    assert done[0] == G1_STEPS

            def z_low(m, t, u):
                big = m * CH + UN * t + u
                z_waits(dve, m, t, u)
                dve.wait_ge(zl_done, big + 1)
                dve_.tensor_scalar(z32[:, u % 2], xt[:, u, 1:BL + 1, :], col(M1), col(R1), ALU.subtract, ALU.mult
                                   ).then_inc(z32_done, 1)
                dve.wait_ge(z32_done, big + 1)
                dve.wait_ge(zh_done, big + 1)
                dve_.tensor_tensor(zl[:, u % 2, 1:BL + 1, 1:W + 1], z32[:, u % 2],
                                   zh[:, u % 2, 1:BL + 1, 1:W + 1], ALU.subtract).then_inc(zl_done, 1)

            for stage in range(5):
                gn1(0, stage)
            z_low(0, 0, 0)
            z_low(0, 0, 1)
            with dve.Fori(0, SA // 2) as t:
                for u in range(2):
                    chunk_stats(1, 2 * t + u, u, t + 1)

            def phase(n, mix, conv, stats):
                m = n + 1

                def add(t, u):
                    j = UN * t + u
                    dve.wait_ge(gelu_done, n * CH + j + 2)
                    dve.wait_ge(r_in[loaded(n, u)], 32 * (TI * n + t + 1))
                    dve_.scalar_tensor_tensor(result(n, u), result(n, u), col(B0), x1[:, bass.ds(j * BL + 1, BL), :],
                                              ALU.add, ALU.add).then_inc(sum_done, 1)

                def conv_out(t, u):
                    j = UN * t + u
                    tail = static(t) and j == CH - 1
                    if mix:
                        dve.wait_ge(sum_done, n * CH + j + 2)
                    dve.wait_ge(conv_done, m * CH + j + 3)
                    s = slice(0, 64), slice(64, 128)
                    for g in range(2):
                        for par in range(2):
                            h = s[par]
                            a = 2 * g + 1 - par
                            ins = dve_.scalar_tensor_tensor(
                                x1[h, bass.ds(j * BL + a, 2), :],
                                ps[h, conv_bank(t, u) + g, 0:N].rearrange("p (r w) -> p r w", r=2),
                                v[h, SOUT:SOUT + 1], xt[h, u, a:a + 2, :], ALU.mult, ALU.add)
                    if tail:
                        ins = dve_.scalar_tensor_tensor(x1[s[1], NB, :], ps[s[1], 6, 0:W], v[s[1], SOUT:SOUT + 1],
                                                        xt[s[1], u, BL, :], ALU.mult, ALU.add)
                    ins.then_inc(evac_done, 1)
                    if not (static(t) and j == 0):
                        if static(t) and j == 1:
                            x1_stats(0, 0, False)
                        x1_stats(t, u, tail)

                def x1_stats(t, u, tail):
                    j = UN * t + u
                    dve.wait_ge(evac_done, m * CH + j + 3)
                    for r in range(2):
                        ins = dve_.bn_stats(st2[:, bass.ds(2 * j + r, 1), :].rearrange("p a s -> p (a s)"),
                                            x1[:, bass.ds(j * BL + 2 * r, 2), :])
                    if tail:
                        ins.then_inc(st2_done, 1)
                        dve.wait_ge(st2_done, 2 * m + 1)
                        dve_.bn_stats(st2[:, 0, :], x1[:, 1:NB + 1:NB - 1, :]).then_inc(st2_done, 1)

                def step(t, u):
                    j = UN * t + u
                    if conv:
                        if not (static(t) and j >= CH - 2):
                            z_low(m, t + (u + 2) // UN, (u + 2) % UN)
                        elif stats and j == CH - 2:
                            z_low(m + 1, 0, 0)
                    if stats and not (static(t) and j >= CH - SA):
                        chunk_stats(m + 1, j + SA, u % 2, SA // 2 + 2 * t + u // 2 + 1)
                    if mix:
                        add(t, u)
                    if conv:
                        conv_out(t, u)
                    if stats and static(t):
                        at = {CH - SA: [0], CH - SA + 2: [1], CH - SA + 4: [2], CH - 3: [3, 4]}
                        for stage in at.get(j, []):
                            gn1(m + 1, stage)
                    if not mix and static(t):
                        k = j - SUMS - 1
                        if 0 <= k < PAIRS:
                            dve.wait_ge(prep_pe, 2 + k)
                            for e in range(2):
                                c = 2 * k + e
                                ins = dve_.tensor_scalar(vsum(c)[0:1], ps[0:1, 4 + k % 2, e * H:(e + 1) * H],
                                                         bhv[:, 0, c:c + 1], bhv[:, 1, c:c + 1], ALU.mult, ALU.add)
                            ins.then_inc(prep, 1)
                        if k == PAIRS + 1:
                            dve.wait_ge(prep_pe, 2 + PAIRS)
                            dve_.tensor_copy(dbias[:].rearrange("p c m -> p (c m)"), ps[0:HH, 6, BIAS:BIAS + 2 * SPLIT])

                steps(dve, step, peel_first=True)

            def between(n, conv, stats):
                base = G2_STEPS * n
                done = [0]

                def link(ins):
                    done[0] += 1
                    ins.then_inc(g2_step, 1)
                    dve.wait_ge(g2_step, base + done[0])

                dve.wait_ge(st2_done, 2 * n + 2)
                dve_.memset(col(GATE2), 0.0)
                link(dve_.bn_aggr(mv[:, 1, :], st2[:]))
                link(dve_.tensor_tensor(mv[:, 1, 0:1], mv[:, 1, 0:1], col(B0), ALU.add))
                link(spread(link, g2_mm, G2_MMS * n + 1, mv[:, 1, :], 2, MU2, DM2, SQ2, VE2))
                link(dve_.tensor_tensor(col(T0), col(B0), col(MU2), ALU.subtract))
                dve.wait_ge(g2_mm, G2_MMS * n + 2)
                link(dve_.tensor_scalar(col(VE2), ps[:, 7, 3:4], 1e-5, None, ALU.add))
                dve.wait_ge(g2_pow, n + 1)
                newton(link, VE2, R02, NT2)
                link(dve_.tensor_tensor(col(T1), col(T0), col(R02), ALU.mult))
                dve_.tensor_scalar(bcin[:, 0:SPLIT], pick_sb[:], col(R02), None, ALU.mult)
                dve_.tensor_scalar(bcin[:, SPLIT:2 * SPLIT], pick_sb[:], col(T1), None, ALU.mult)
                dve_.tensor_tensor(col(SH2), col(T1), sel[:, 1:2], ALU.mult)
                link(dve_.scalar_tensor_tensor(col(RS2), col(R02), sel[:, 1:2], sel[:, 0:1], ALU.mult, ALU.add))
                link(dve_.tensor_scalar(w1n[:], w1bd[:], col(RS2), None, ALU.mult))
                dve.wait_ge(g2_mm, G2_MMS * n + 4)
                dve_.tensor_tensor(col(BU), ps[:, 7, 4:5], col(B1), ALU.add)
                dve_.tensor_copy(bc[:], ps[:, 7, 8:8 + 2 * SPLIT]).then_inc(g2_step, 1)
                assert done[0] + 1 == G2_STEPS, done

                def plane_out(q, u):
                    c = 4 * q + u
                    dve.wait_ge(vb_done, n * SPLIT + c + 5)
                    dve.wait_ge(d_out[u], 1 + 16 * (QS * n + q))
                    bias = dbias[:, bass.ds(c, 1), :].rearrange("p a m -> p (a m)").rearrange("p (m a) -> p m a", a=1)
                    dve_.tensor_tensor(dt_[:, u], ps[0:HH, 6 + u % 2, 0:N].rearrange("p (m w) -> p m w", m=2),
                                       bias.broadcast_to([HH, 2, W]), ALU.add).then_inc(dw_done, 1)

                if conv:
                    z_low(n + 1, 0, 1)
                with dve.Fori(0, QS) as q:
                    for u in range(4):
                        plane_out(q, u)
                        if stats and u % 2:
                            chunk_stats(n + 2, 2 * q + u // 2, u // 2, q + 1)

            images(dve, phase, between)


def kernel(**inputs):
    import numpy as _np
    import concourse.bacc as _bacc
    from concourse.bass_utils import run_bass_kernel_spmd as _run

    x = _np.ascontiguousarray(inputs["x"])
    w = _np.asarray(inputs["L0_conv_weight"])
    C = w.shape[0]
    split, taps = inputs["L1_conv_w_1xk"].shape[0], inputs["L1_conv_w_1xk"].shape[3]
    ch = _np.arange(2 * C) % C
    sel = (ch < split)
    arrays = {
        "x": x,
        "w_co": w.reshape(C, -1),
        "w_ci": w.transpose(1, 2, 3, 0).reshape(C, -1, C),
        "bias0": inputs["L0_conv_bias"].reshape(C, 1),
        "cmask": _np.asarray(inputs["L0_conv_channel_mask"]).view(_np.int32).reshape(1, -1),
        "imask": _np.asarray(inputs["L0_conv_input_channel_mask"]).view(_np.int32).reshape(1, -1),
        "k_v": inputs["L1_conv_w_kx1"].reshape(split, taps)[:, ::-1],
        "k_h": inputs["L1_conv_w_1xk"].reshape(split, taps)[:, ::-1],
        "b_h": inputs["L1_conv_b_1xk"].reshape(1, split),
        "b_v": inputs["L1_conv_b_kx1"].reshape(1, split),
        "w1t": inputs["L1_conv_w1"].reshape(C, C).T,
        "b1": inputs["L1_conv_b1"].reshape(C, 1),
        "ident": _np.eye(C, dtype=_np.float32),
        "group_avg": (0.25 * (ch[:, None] // 2 == ch[None, :] // 2)).astype(_np.float32),
        "pick": _np.eye(2 * C, split, dtype=_np.float32),
        "x1_sel": _np.stack([sel, ~sel], 1).astype(_np.float32),
    }
    arrays = {k: _np.ascontiguousarray(a) for k, a in arrays.items()}
    nc = _bacc.Bacc("TRN2", target_bir_lowering=False, num_devices=1)
    args = [nc.dram_tensor(f"in_{k}", a.shape, mybir.dt.from_np(a.dtype), kind="ExternalInput").ap()
            for k, a in arrays.items()]
    args.append(nc.dram_tensor("out_y", x.shape, F32, kind="ExternalOutput").ap())
    conv_preact_kernel(nc, *args)
    r = _run(nc, [{f"in_{k}": a for k, a in arrays.items()}], core_ids=[0])
    return r.results[0]["out_y"]
```
